# Optimizing a Trainium2 kernel written in Bass

```python
import numpy as np
import jax
import jax.numpy as jnp

def _softmax(x, axis=-1):
    return jax.nn.softmax(x, axis=axis)

def _gelu(x):
    return jax.nn.gelu(x, approximate=True)

def _silu(x):
    return jax.nn.silu(x)

def _sigmoid(x):
    return jax.nn.sigmoid(x)

def _layernorm(x, axis=-1, eps=1e-05):
    m = jnp.mean(x, axis=axis, keepdims=True)
    v = jnp.var(x, axis=axis, keepdims=True)
    return (x - m) / jnp.sqrt(v + eps)

def _scatter_add(tgt, idx, src, axis=0):
    return tgt.at[idx].add(src)

def _segment_sum(src, seg, n):
    return jax.ops.segment_sum(src, seg, n)
kernel_name = 'mk_adj_resnorm_d4_adj_r2_5b01b1'

def setup_inputs(seed: int=0):
    np.random.seed(seed)
    _w = jnp.asarray

    def _rec_inputs():
        import jax
        import jax.numpy as jnp
        _gk = jax.random.key(seed)
        x = -0.0005207 + 1.001 * jax.random.normal(jax.random.fold_in(_gk, 1), (16, 512, 128), jnp.float32)
        _a = jax.random.bernoulli(jax.random.fold_in(_gk, 2), 0.00390625, (16, 512, 512))
        adj = _a.astype(jnp.int32)
        return (x, adj)
    x, adj = _rec_inputs()

    def _L0_gnn_setup():
        import jax, jax.numpy as jnp
        import numpy as np
        DIM = 128
        HEADS = 8
        HEAD_DIM = DIM // HEADS
        DFF = 4 * DIM
        EPS = 1e-05

        def _layernorm(x, g, b):
            m = jnp.mean(x, axis=-1, keepdims=True)
            v = jnp.mean(jnp.square(x - m), axis=-1, keepdims=True)
            return (x - m) * jax.lax.rsqrt(v + EPS) * g + b
        key = jax.random.key(seed)
        ks = jax.random.split(key, 12)
        B, N = (8, 512)
        s = 1.0 / np.sqrt(DIM)
        x = jax.random.normal(ks[0], (B, N, DIM), dtype=jnp.float32)
        adj = jax.random.randint(ks[1], (B, N, N), 0, 2, dtype=jnp.int32)
        return {'x': x, 'adj': adj, 'Wqkv': jax.random.normal(ks[2], (3 * DIM, DIM), jnp.float32) * s, 'bqkv': jnp.zeros((3 * DIM,), jnp.float32), 'Wo': jax.random.normal(ks[3], (DIM, DIM), jnp.float32) * s, 'bo': jnp.zeros((DIM,), jnp.float32), 'ln1_g': jnp.ones((DIM,), jnp.float32), 'ln1_b': jnp.zeros((DIM,), jnp.float32), 'W1': jax.random.normal(ks[4], (DFF, DIM), jnp.float32) * s, 'b1': jnp.zeros((DFF,), jnp.float32), 'W2': jax.random.normal(ks[5], (DIM, DFF), jnp.float32) * (1.0 / np.sqrt(DFF)), 'b2': jnp.zeros((DIM,), jnp.float32), 'ln2_g': jnp.ones((DIM,), jnp.float32), 'ln2_b': jnp.zeros((DIM,), jnp.float32)}
    _L0_gnn_all = _L0_gnn_setup()
    _L0_gnn_in = {k: v for k, v in _L0_gnn_all.items() if k in ('Wqkv', 'bqkv', 'Wo', 'bo', 'ln1_g', 'ln1_b', 'W1', 'b1', 'W2', 'b2', 'ln2_g', 'ln2_b')}
    del _L0_gnn_all

    def _L1_gnn_setup():
        import jax, jax.numpy as jnp
        import numpy as np
        ALPHA = 0.2
        NEG_BIG = -9000000000000000.0
        key = jax.random.key(seed)
        k1, k2, k3, k4 = jax.random.split(key, 4)
        B, N, F_in, F_out = (16, 512, 128, 128)
        x = jax.random.normal(k1, (B, N, F_in), dtype=jnp.float32)
        adj = jax.random.randint(k2, (B, N, N), 0, 2, dtype=jnp.int32)
        W = jax.random.normal(k3, (F_in, F_out), dtype=jnp.float32) * np.sqrt(2.0 / (F_in + F_out))
        a = jax.random.normal(k4, (2 * F_out, 1), dtype=jnp.float32) * np.sqrt(2.0 / (2 * F_out + 1))
        return {'x': x, 'adj': adj, 'W': W, 'a': a}
    _L1_gnn_all = _L1_gnn_setup()
    _L1_gnn_in = {k: v for k, v in _L1_gnn_all.items() if k in ('W', 'a')}
    del _L1_gnn_all

    def _L2_gnn_setup():
        import jax, jax.numpy as jnp
        import numpy as np
        B, N, D_IN, D_OUT, R = (8, 1024, 128, 128, 4)
        key = jax.random.key(seed)
        k1, k2, k3, k4 = jax.random.split(key, 4)
        x = jax.random.normal(k1, (B, N, D_IN), dtype=jnp.float32)
        adj = jnp.zeros((1,), dtype=jnp.float32)
        relation = jax.random.randint(k2, (B, N, N), 0, R + 1, dtype=jnp.int32)
        weight = jax.random.normal(k3, (R, D_IN, D_OUT), dtype=jnp.float32) * 0.05
        bias = jax.random.normal(k4, (D_OUT,), dtype=jnp.float32) * 0.05
        return {'x': x, 'adj': adj, 'relation': relation, 'weight': weight, 'bias': bias}
    _L2_gnn_all = _L2_gnn_setup()
    _L2_gnn_in = {k: v for k, v in _L2_gnn_all.items() if k in ('adj', 'weight', 'bias')}
    del _L2_gnn_all

    def _L3_gnn_setup():
        import jax, jax.numpy as jnp
        import numpy as np
        BS, N, D, R = (16, 256, 128, 2)
        key = jax.random.key(seed)
        ks = jax.random.split(key, 9)
        s = 1.0 / np.sqrt(D)
        return {'encoded_spans': jax.random.normal(ks[0], (BS, N, D), dtype=jnp.float32), 'w_rel1': jax.random.normal(ks[1], (R, D, D), dtype=jnp.float32) * s, 'w_root1': jax.random.normal(ks[2], (D, D), dtype=jnp.float32) * s, 'b1': jnp.zeros((D,), dtype=jnp.float32), 'w_rel2': jax.random.normal(ks[3], (R, D, D), dtype=jnp.float32) * s, 'w_root2': jax.random.normal(ks[4], (D, D), dtype=jnp.float32) * s, 'b2': jnp.zeros((D,), dtype=jnp.float32), 'aug_adj': jax.random.randint(ks[5], (BS, N, N), 0, 16, dtype=jnp.int64), 'punct_graph': jax.random.randint(ks[6], (BS, N, N), 0, 16, dtype=jnp.int64)}
    _L3_gnn_all = _L3_gnn_setup()
    _L3_gnn_in = {k: v for k, v in _L3_gnn_all.items() if k in ('w_rel1', 'w_root1', 'b1', 'w_rel2', 'w_root2', 'b2')}
    del _L3_gnn_all
    return {'x': x, 'adj': adj, 'L0_gnn_Wqkv': _L0_gnn_in['Wqkv'], 'L0_gnn_bqkv': _L0_gnn_in['bqkv'], 'L0_gnn_Wo': _L0_gnn_in['Wo'], 'L0_gnn_bo': _L0_gnn_in['bo'], 'L0_gnn_ln1_g': _L0_gnn_in['ln1_g'], 'L0_gnn_ln1_b': _L0_gnn_in['ln1_b'], 'L0_gnn_W1': _L0_gnn_in['W1'], 'L0_gnn_b1': _L0_gnn_in['b1'], 'L0_gnn_W2': _L0_gnn_in['W2'], 'L0_gnn_b2': _L0_gnn_in['b2'], 'L0_gnn_ln2_g': _L0_gnn_in['ln2_g'], 'L0_gnn_ln2_b': _L0_gnn_in['ln2_b'], 'L1_gnn_W': _L1_gnn_in['W'], 'L1_gnn_a': _L1_gnn_in['a'], 'L2_gnn_adj': _L2_gnn_in['adj'], 'L2_gnn_weight': _L2_gnn_in['weight'], 'L2_gnn_bias': _L2_gnn_in['bias'], 'L3_gnn_w_rel1': _L3_gnn_in['w_rel1'], 'L3_gnn_w_root1': _L3_gnn_in['w_root1'], 'L3_gnn_b1': _L3_gnn_in['b1'], 'L3_gnn_w_rel2': _L3_gnn_in['w_rel2'], 'L3_gnn_w_root2': _L3_gnn_in['w_root2'], 'L3_gnn_b2': _L3_gnn_in['b2']}

def reference(x, adj, L0_gnn_Wqkv, L0_gnn_bqkv, L0_gnn_Wo, L0_gnn_bo, L0_gnn_ln1_g, L0_gnn_ln1_b, L0_gnn_W1, L0_gnn_b1, L0_gnn_W2, L0_gnn_b2, L0_gnn_ln2_g, L0_gnn_ln2_b, L1_gnn_W, L1_gnn_a, L2_gnn_adj, L2_gnn_weight, L2_gnn_bias, L3_gnn_w_rel1, L3_gnn_w_root1, L3_gnn_b1, L3_gnn_w_rel2, L3_gnn_w_root2, L3_gnn_b2):
    import jax
    import jax.numpy as jnp

    def _L0_gnn_ref(x, adj, Wqkv, bqkv, Wo, bo, ln1_g, ln1_b, W1, b1, W2, b2, ln2_g, ln2_b):
        import jax, jax.numpy as jnp
        import numpy as np
        DIM = 128
        HEADS = 8
        HEAD_DIM = DIM // HEADS
        DFF = 4 * DIM
        EPS = 1e-05

        def _layernorm(x, g, b):
            m = jnp.mean(x, axis=-1, keepdims=True)
            v = jnp.mean(jnp.square(x - m), axis=-1, keepdims=True)
            return (x - m) * jax.lax.rsqrt(v + EPS) * g + b
        B, N, _ = x.shape
        eye = jnp.eye(N, dtype=bool)[None]
        allowed = (adj > 0) | (jnp.swapaxes(adj, 1, 2) > 0) | eye
        qkv = x @ Wqkv.T + bqkv
        q, k, v = jnp.split(qkv, 3, axis=-1)

        def heads(t):
            return t.reshape(B, N, HEADS, HEAD_DIM).transpose(0, 2, 1, 3)
        q, k, v = (heads(q), heads(k), heads(v))
        scale = 1.0 / np.sqrt(HEAD_DIM)
        scores = jnp.einsum('bhqd,bhkd->bhqk', q * scale, k)
        scores = jnp.where(allowed[:, None], scores, -jnp.inf)
        attn = jax.nn.softmax(scores, axis=-1)
        ctx = jnp.einsum('bhqk,bhkd->bhqd', attn, v)
        ctx = ctx.transpose(0, 2, 1, 3).reshape(B, N, DIM)
        attn_out = ctx @ Wo.T + bo
        x = _layernorm(x + attn_out, ln1_g, ln1_b)
        ff = jax.nn.relu(x @ W1.T + b1) @ W2.T + b2
        x = _layernorm(x + ff, ln2_g, ln2_b)
        return x

    def _L1_gnn_ref(x, adj, W, a):
        import jax, jax.numpy as jnp
        import numpy as np
        ALPHA = 0.2
        NEG_BIG = -9000000000000000.0
        F_out = a.shape[0] // 2
        h = jnp.einsum('bni,io->bno', x, W)
        a_l = a[:F_out, 0]
        a_r = a[F_out:, 0]
        el = h @ a_l
        er = h @ a_r
        e = jax.nn.leaky_relu(el[:, :, None] + er[:, None, :], ALPHA)
        e = jnp.where(adj > 0, e, NEG_BIG)
        attn = jax.nn.softmax(e, axis=-1)
        return jnp.einsum('bij,bjo->bio', attn, h)

    def _L2_gnn_ref(x, adj, relation, weight, bias):
        import jax, jax.numpy as jnp
        import numpy as np
        B, N, D_IN, D_OUT, R = (8, 1024, 128, 128, 4)
        rel_ids = jnp.arange(1, weight.shape[0] + 1, dtype=relation.dtype)
        masks = (relation[None] == rel_ids[:, None, None, None]).astype(x.dtype)
        h = jnp.einsum('rbnm,bmd->rbnd', masks, x)
        y = jnp.einsum('rbnd,rdo->bno', h, weight)
        return y + bias

    def _L3_gnn_ref(encoded_spans, w_rel1, w_root1, b1, w_rel2, w_root2, b2, aug_adj, punct_graph):
        import jax, jax.numpy as jnp
        import numpy as np
        BS, N, D, R = (16, 256, 128, 2)
        mask_punct = (punct_graph == 1) & (aug_adj != 1)
        mask_aug = aug_adj == 1
        masks = jnp.stack([mask_punct, mask_aug]).astype(encoded_spans.dtype)
        deg = jnp.maximum(masks.sum(axis=2), 1.0)[..., None]

        def conv(x, w_rel, w_root, b):
            out = jnp.einsum('bnd,de->bne', x, w_root) + b
            for r in range(R):
                agg = jnp.einsum('bij,bid->bjd', masks[r], x) / deg[r]
                out = out + jnp.einsum('bjd,de->bje', agg, w_rel[r])
            return out
        h = jax.nn.elu(conv(encoded_spans, w_rel1, w_root1, b1))
        h = jax.nn.elu(conv(h, w_rel2, w_root2, b2))
        return h
    x = _layernorm(x + _L0_gnn_ref(x, adj, L0_gnn_Wqkv, L0_gnn_bqkv, L0_gnn_Wo, L0_gnn_bo, L0_gnn_ln1_g, L0_gnn_ln1_b, L0_gnn_W1, L0_gnn_b1, L0_gnn_W2, L0_gnn_b2, L0_gnn_ln2_g, L0_gnn_ln2_b), axis=-1)
    x = _layernorm(x + _L1_gnn_ref(x, adj, L1_gnn_W, L1_gnn_a), axis=-1)
    x = _layernorm(x + _L2_gnn_ref(x, L2_gnn_adj, adj, L2_gnn_weight, L2_gnn_bias), axis=-1)
    x = _layernorm(x + _L3_gnn_ref(x, L3_gnn_w_rel1, L3_gnn_w_root1, L3_gnn_b1, L3_gnn_w_rel2, L3_gnn_w_root2, L3_gnn_b2, adj, adj), axis=-1)
    return x

_drawn_inputs = setup_inputs


def setup_inputs(seed=0):
    import zlib

    import numpy as np

    out = dict(_drawn_inputs(seed))
    spreads = {'L0_gnn_bqkv': (0.0, 0.1),
     'L0_gnn_bo': (0.0, 0.1),
     'L0_gnn_ln1_g': (1.0, 0.2),
     'L0_gnn_ln1_b': (0.0, 0.1),
     'L0_gnn_b1': (0.0, 0.1),
     'L0_gnn_b2': (0.0, 0.1),
     'L0_gnn_ln2_g': (1.0, 0.2),
     'L0_gnn_ln2_b': (0.0, 0.1),
     'L3_gnn_b1': (0.0, 0.1),
     'L3_gnn_b2': (0.0, 0.1)}
    factors = {}
    for name, (base, spread) in spreads.items():
        noise = np.random.default_rng([zlib.crc32(name.encode()), seed]).standard_normal(out[name].shape)
        drawn = base * np.exp(spread * noise) if base else spread * noise
        out[name] = jnp.asarray(drawn.astype(out[name].dtype))
    for name, factor in factors.items():
        out[name] = (out[name] * factor).astype(out[name].dtype)
    return out
```

```python
from contextlib import ExitStack

import concourse.bass as bass
from concourse import mybir

ALU = mybir.AluOpType
ACT = mybir.ActivationFunctionType
F32 = mybir.dt.float32
F32R = mybir.dt.float32r
F16 = mybir.dt.float16
BF16 = mybir.dt.bfloat16
I32 = mybir.dt.int32

GRAPHS, NODES, DIM = 16, 512, 128
P = 128
TILES = NODES // P
HEADS = 8
HEAD = DIM // HEADS
GROUP = 4
GROUPS = HEADS // GROUP
SLOT = 32
DFF = 4 * DIM
FT = DFF // P
RELS = 4
EPS = 1e-5
SCALE = 1.0 / HEAD ** 0.5
NEVER = -1e30
NEG_BIG = -9e15
ALPHA = 0.2
UP = 4096.0
PACK = 64
ONE_ROW, SHIFT_ROW = PACK, PACK + 1

W_COLS = {}
_at = 0
for _n, _w in (("q", P), ("k", P), ("v", P), ("o", P), ("ff1", DFF), ("ff2", DFF), ("gat", P), ("gatT", P),
               ("rel", RELS * P), ("root1", P), ("near1", P), ("root2", P), ("near2", P), ("ident", P)):
    W_COLS[_n] = (_at, _at + _w)
    _at += _w
W_ALL = _at

VECS = ("bq", "bk", "bv", "bo", "g1", "b1", "g2", "b2", "ff1_0", "ff1_1", "ff1_2", "ff1_3", "ff2", "bias", "c1", "c2",
        "a_l", "a_r")
ROWS = ("bv", "bo", "g1", "b1", "g2", "b2", "ff2", "bias", "c1", "c2")

ORDER = (
    ("S", 0), ("early", 0), ("unit", 0), ("S", 1), ("turn_ctx", 0), ("S", 2), ("wo", 0), ("S", 3), ("M", 0),
    ("turn_z", 0), ("S", 4), ("ff1", 0), ("S", 5), ("T", 0), ("ff2", 0), ("T", 1), ("V", 0), ("S", 6),
    ("turn_y1", 0), ("T", 2), ("V", 1), ("S", 7), ("gat_in", 0), ("T", 3), ("V", 2), ("M", 1),
    ("gat_turn", 0), ("V", 3), ("C", 0), ("gat_sum", 0), ("T", 4), ("agg", 0), ("T", 5), ("V", 4),
    ("agg", 1), ("prep", 0), ("proj", 0), ("rel", 0), ("T", 6), ("prep", 1), ("V", 5), ("near1", 0), ("T", 7), ("V", 6), ("conv1", 0),
    ("V", 7), ("C", 1), ("near2", 0), ("conv2", 0),
)


def build(nc, x, xT, adj, adjT, weights, vec_rows, vec_cols, out):
    with ExitStack() as ctx:
        def sb(name, shape, dt=F32):
            return ctx.enter_context(nc.sbuf_tensor(name, shape, dt))

        def sem(name):
            return ctx.enter_context(nc.semaphore(name))

        wts = sb("wts", [P, W_ALL])
        cols = sb("cols", [P, len(VECS)])
        rows = sb("rows", [P, len(ROWS), DIM])
        gat_ext = sb("gat_ext", [P, DIM + 1])
        gat_right = sb("gat_right", [P, P])
        a_right = sb("a_right", [P, P])
        ff_bias = sb("ff_bias", [P, DIM])
        not_self = sb("not_self", [P, P], BF16)
        ones16 = sb("ones16", [P, 2], F16)
        eps_tile = sb("eps_tile", [P, TILES])
        half_tile = sb("half_tile", [P, TILES])

        adj_in = sb("adj_in", [P, TILES, NODES], I32)
        adjT_in = sb("adjT_in", [P, TILES, NODES], I32)
        codes = [sb(f"codes{i}", [P, TILES, NODES], BF16) for i in range(2)]
        codesT = [sb(f"codesT{i}", [P, TILES, NODES], BF16) for i in range(2)]
        barred = [sb(f"barred{i}", [P, TILES, NODES], BF16) for i in range(2)]
        x_nat = sb("x_nat", [P, TILES, DIM])
        x_turned = sb("x_turned", [P, NODES])
        q_hi = sb("q_hi", [P, NODES], F32R)
        q_lo = sb("q_lo", [P, NODES], F32R)
        k_hi = sb("k_hi", [P, NODES], F32R)
        k_lo = sb("k_lo", [P, NODES], F32R)
        q_pack = sb("q_pack", [SHIFT_ROW + 1, HEADS, NODES], F32R)
        k_pack = sb("k_pack", [SHIFT_ROW + 1, HEADS, NODES], F32R)
        values = [sb(f"values{i}", [P, TILES, HEADS, SLOT]) for i in range(2)]
        maxima = sb("maxima", [P, HEADS * TILES])
        shift = sb("shift", [GROUP * TILES, P], F32R)
        probs = [sb(f"probs{i}", [P, GROUP, NODES]) for i in range(4)]
        ctx_T = [sb(f"ctx_T{i}", [P, NODES]) for i in range(GROUPS)]

        ctx_sum = sb("ctx_sum", [P, TILES * HEADS])
        ctx_nat = sb("ctx_nat", [P, TILES, DIM])
        turned_a = sb("turned_a", [P, NODES])
        turned_b = sb("turned_b", [P, NODES])
        big_a = sb("big_a", [P, TILES, NODES])
        big_b = sb("big_b", [P, TILES, NODES])
        n_a = sb("n_a", [P, TILES, DIM])
        n_b = sb("n_b", [P, TILES, DIM])
        n_c = sb("n_c", [P, TILES, DIM])
        n_d = sb("n_d", [P, TILES, DIM])
        n_e = sb("n_e", [P, TILES, DIM])
        n_f = sb("n_f", [P, TILES, DIM])
        resid = sb("resid", [P, TILES, DIM])
        result = sb("result", [P, TILES, DIM])
        stats = sb("stats", [P, TILES, 6])
        moments = sb("moments", [P, TILES, 2])
        spread = sb("spread", [P, TILES])
        rstd = sb("rstd", [P, TILES])
        no_edge = sb("no_edge", [P, TILES, NODES], BF16)
        is_one = sb("is_one", [P, TILES, NODES], F16)
        is_rel = [sb(f"is_rel{i}", [P, TILES, NODES], F16) for i in range(2)]
        h_ext = sb("h_ext", [P, TILES, DIM + 1])
        gat_max = sb("gat_max", [P, TILES])
        gat_top = sb("gat_top", [P, TILES])
        gat_low = sb("gat_low", [P, TILES])
        gat_total = sb("gat_total", [P, TILES])
        gat_inv = sb("gat_inv", [P, TILES])
        degree = sb("degree", [P, TILES])
        deg_inv = sb("deg_inv", [P, TILES])
        part_hi = sb("part_hi", [P, TILES, DIM], F16)
        part_lo = sb("part_lo", [P, TILES, DIM], F16)
        h_parts = [is_rel[0][:, i, :].bitcast(BF16).rearrange("p (t c) -> p t c", t=TILES) for i in range(3)]

        S_bank = [ctx.enter_context(nc.psum_tensor(f"S_bank{i}", [P, 512], F32)) for i in range(2)]
        T_bank = [ctx.enter_context(nc.psum_tensor(f"T_bank{i}", [P, 512], F32)) for i in range(2)]
        C_bank = ctx.enter_context(nc.psum_tensor("C_bank", [P, 512], F32))
        X_pair = ctx.enter_context(nc.psum_tensor("X_pair", [P, 2, 512], F32))
        X_last = ctx.enter_context(nc.psum_tensor("X_last", [P, 512], F32))
        X = [X_pair[:, 0, :], X_pair[:, 1, :], X_last[:, :]]

        bounce = [nc.dram_tensor(f"bounce{i}", [4, P, NODES], F32).ap() for i in range(2)]

        def w(name, a=0, b=None):
            lo, hi = W_COLS[name]
            return wts[:, lo + a:(hi if b is None else lo + b)]

        def col(name):
            n = VECS.index(name)
            return cols[:, n:n + 1]

        def row4(name):
            return rows[:, ROWS.index(name):ROWS.index(name) + 1, :].broadcast_to((P, TILES, DIM))

        def nat(bank):
            return bank.rearrange("p (t c) -> p t c", t=TILES)

        weights_in = sem("weights_in")
        values_zeroed = sem("values_zeroed")
        dve_consts = sem("dve_consts")
        pool_consts = sem("pool_consts")
        ff_bias_ready = sem("ff_bias_ready")
        gat_a_ready = sem("gat_a_ready")
        gat_w_psum = sem("gat_w_psum")
        gat_w_ready = sem("gat_w_ready")
        adj_in_sem = sem("adj_in_sem")
        x_in = sem("x_in")
        xT_in = sem("xT_in")
        coded = sem("coded")
        allow = sem("allow")
        qk_proj = sem("qk_proj")
        qk_hi = sem("qk_hi")
        qk_lo = sem("qk_lo")
        v_proj = sem("v_proj")
        v_ready = sem("v_ready")
        bounced = sem("bounced")
        packed = [sem(f"packed{i}") for i in range(GROUPS)]
        scored = sem("scored")
        maxed = sem("maxed")
        max_turned = sem("max_turned")
        shift_ready = sem("shift_ready")
        shift_packed = sem("shift_packed")
        shifted = sem("shifted")
        barred_out = sem("barred_out")
        exped = sem("exped")
        weighted = sem("weighted")
        ctx_copied = sem("ctx_copied")
        gate = sem("gate")

        ctx_turned = sem("ctx_turned")
        ctx_inv = sem("ctx_inv")
        ctx_scaled = sem("ctx_scaled")
        ctx_back = sem("ctx_back")
        ctx_back_in = sem("ctx_back_in")
        x_bo = sem("x_bo")
        x_b2 = sem("x_b2")
        wo_done = sem("wo_done")
        resid_ready = sem("resid_ready")
        stats_ready = sem("stats_ready")
        moments_ready = sem("moments_ready")
        spread_ready = sem("spread_ready")
        rstd_ready = sem("rstd_ready")
        normed = sem("normed")
        z_turned = sem("z_turned")
        z_in = sem("z_in")
        z_scaled = sem("z_scaled")
        x1_ready = sem("x1_ready")
        ff1_done = sem("ff1_done")
        ff1_in = sem("ff1_in")
        ff2_done = sem("ff2_done")
        z2_scaled = sem("z2_scaled")
        y1_turned = sem("y1_turned")
        y1_in = sem("y1_in")
        gat_right_done = sem("gat_right_done")
        h_done = sem("h_done")
        h_in = sem("h_in")
        no_edge_ready = sem("no_edge_ready")
        gat_maxed = sem("gat_maxed")
        gat_sum_max = sem("gat_sum_max")
        gat_top_ready = sem("gat_top_ready")
        gat_low_ready = sem("gat_low_ready")
        gat_e = sem("gat_e")
        gat_leaky = sem("gat_leaky")
        gat_exped = sem("gat_exped")
        gat_pT = sem("gat_pT")
        gat_pT_in = sem("gat_pT_in")
        gat_done = sem("gat_done")
        gat_inv_ready = sem("gat_inv_ready")
        hi_ready = sem("hi_ready")
        lo_ready = sem("lo_ready")
        y2_bias = sem("y2_bias")
        rel_mask = sem("rel_mask")
        agg_done = sem("agg_done")
        agg_in = sem("agg_in")
        rel_done = sem("rel_done")
        one_mask = sem("one_mask")
        y3_turned = sem("y3_turned")
        y3_in = sem("y3_in")
        near_done = sem("near_done")
        near_in = sem("near_in")
        deg_done = sem("deg_done")
        deg_ready = sem("deg_ready")
        deg_inv_ready = sem("deg_inv_ready")
        root_done = sem("root_done")
        near_w_done = sem("near_w_done")
        root_in = sem("root_in")
        pre_ready = sem("pre_ready")
        pre_low = sem("pre_low")
        pre_exp = sem("pre_exp")
        elu_ready = sem("elu_ready")
        part1 = sem("part1")
        rest1 = sem("rest1")
        part2 = sem("part2")
        part3 = sem("part3")
        h1_turned = sem("h1_turned")
        h1_in = sem("h1_in")
        stored = sem("stored")

        def first(g):
            return isinstance(g, int) and g == 0

        def alone(eng, s, value):
            eng.wait_ge(s, value)
            eng.sem_inc(gate, 1)

        S_USES = ["tile"] * (TILES * GROUP) + ["max"] + ["tile"] * (TILES * GROUP) + ["max"]

        def wait_S_bank(eng, g, n):
            m = (n - 2) % len(S_USES)
            if n < 2 and first(g):
                return
            back = 0 if n >= 2 else 1
            done = S_USES[:m + 1].count(S_USES[m])
            if S_USES[m] == "tile":
                eng.wait_ge(maxed, g * 32 + (done - 32 * back))
            else:
                eng.wait_ge(shift_ready, g * 2 + (done - 2 * back))

        def S_use(h, t):
            return h * TILES + t + (1 if h >= GROUP else 0)

        def steps(eng, step):
            step(0, 0, None, 0, 1)
            step(1, 1, 0, 1, 2)
            with eng.Fori(0, (GRAPHS - 4) // 2) as n:
                i = n * 2 + 2
                step(i, 0, i - 1, i, i + 1)
                step(i + 1, 1, i, i + 1, i + 2)
            step(GRAPHS - 2, 0, GRAPHS - 3, GRAPHS - 2, GRAPHS - 1)
            step(GRAPHS - 1, 1, GRAPHS - 2, GRAPHS - 1, None)
            step(GRAPHS, 0, GRAPHS - 1, None, None)

        block = ctx.enter_context(nc.Block())

        @block.sync
        def _(sp):
            sp.dma_start(wts[:, :], weights).then_inc(weights_in, 16)
            sp.dma_start(cols[:, :], vec_cols).then_inc(weights_in, 16)
            sp.dma_start(rows[:, :, :].rearrange("p a b -> p (a b)"),
                         vec_rows.partition_broadcast(P)).then_inc(weights_in, 16)

            def load_adj(g):
                sp.dma_start(adj_in[:, :, :].rearrange("p t n -> p (t n)"), adj[g]).then_inc(adj_in_sem, 16)
                sp.dma_start(adjT_in[:, :, :].rearrange("p t n -> p (t n)"), adjT[g]).then_inc(adj_in_sem, 16)

            def bounce_out(g, p):
                for n, (s, src) in enumerate(((qk_hi, q_hi), (qk_lo, q_lo), (qk_hi, k_hi), (qk_lo, k_lo))):
                    sp.wait_ge(s, g * 2 + 1 + n // 2)
                    sp.dma_start(bounce[p][n], src[:, :].bitcast(F32)).then_inc(bounced, 16)

            def pack(g, p, grp):
                sp.wait_ge(bounced, g * 64 + 64)
                if not first(g):
                    sp.wait_ge(shifted, g * 32 + (16 * (grp + 1) - 32))
                for dst, parts in ((q_pack, (0, 0, 1, 1)), (k_pack, (2, 3, 2, 3))):
                    for b, part in enumerate(parts):
                        src = bounce[p][part].rearrange("(h d) n -> d h n", h=HEADS)
                        sp.dma_start(dst[b * HEAD:(b + 1) * HEAD, grp * GROUP:(grp + 1) * GROUP, :].bitcast(F32),
                                     src[:, grp * GROUP:(grp + 1) * GROUP, :]).then_inc(packed[grp], 16)

            sp.dma_start(x_turned[:, :], xT[0]).then_inc(xT_in, 16)
            load_adj(0)
            bounce_out(0, 0)
            sp.wait_ge(v_proj, 1)
            sp.dma_start(x_turned[:, :], xT[1]).then_inc(xT_in, 16)
            sp.wait_ge(coded, 2)
            load_adj(1)
            pack(0, 0, 0)
            sp.wait_ge(dve_consts, 2)
            pack(0, 0, 1)

            def step(i, p, tail, attn, proj):
                for what, n in ORDER:
                    if what == "early" and attn is not None:
                        if not first(attn):
                            sp.wait_ge(x_b2, attn)
                            sp.wait_ge(x_bo, attn)
                        sp.dma_start(x_nat[:, :, :].rearrange("p t c -> p (t c)"), x[attn]).then_inc(x_in, 16)
                    if what == "M" and attn is not None:
                        sp.wait_ge(shift_ready, attn * 2 + (n + 1))
                        sp.dma_start(q_pack[SHIFT_ROW:SHIFT_ROW + 1, n * GROUP:(n + 1) * GROUP, :]
                                     .rearrange("o h (t q) -> o (h t) q", t=TILES).bitcast(F32),
                                     shift[:, :].bitcast(F32)).then_inc(shift_packed, 16)
                    if what == "proj" and proj is not None:
                        bounce_out(proj, 1 - p)
                        if not (isinstance(proj, int) and proj == GRAPHS - 1):
                            sp.wait_ge(v_proj, proj + 1)
                            sp.dma_start(x_turned[:, :], xT[proj + 1]).then_inc(xT_in, 16)
                            sp.wait_ge(coded, proj * 2 + 2)
                            load_adj(proj + 1)
                        pack(proj, 1 - p, 0)
                    if what == "C" and n == 1 and proj is not None:
                        pack(proj, 1 - p, 1)
                if tail is not None:
                    sp.wait_ge(normed, tail * 6 + 6)
                    sp.dma_start(out[tail], result[:, :, :].rearrange("p t c -> p (t c)")).then_inc(stored, 16)

            steps(sp, step)
            sp.wait_ge(stored, 16 * GRAPHS)

        @block.tensor
        def _(pe):
            ident = w("ident")

            pe.wait_ge(weights_in, 48)
            pe.wait_ge(gat_a_ready, 1)
            nc.tensor.matmul(X[1][:, 0:P], w("gatT"), a_right[:, :], start=True, stop=True)
            nc.tensor.matmul(X[1][:, P:P + 1], w("gatT"), col("a_l"), start=True, stop=True).then_inc(gat_w_psum, 1)
            pe.wait_ge(gat_w_ready, 1)

            def project(g):
                pe.wait_ge(xT_in, g * 16 + 16)
                if not (isinstance(g, int) and g < 2):
                    pe.wait_ge(agg_in, g * 4 - 6)
                nc.tensor.matmul(X[0], w("q"), x_turned[:, :], start=True, stop=True).then_inc(qk_proj, 1)
                if not (isinstance(g, int) and g < 2):
                    pe.wait_ge(agg_in, g * 4 - 4)
                nc.tensor.matmul(X[1], w("k"), x_turned[:, :], start=True, stop=True).then_inc(qk_proj, 1)
                for t in range(TILES):
                    last = nc.tensor.matmul(nat(X[2])[:, t, :], x_turned[:, t * P:(t + 1) * P], w("v"),
                                            start=True, stop=True)
                last.then_inc(v_proj, 1)

            project(0)

            def attention(what, n, g, p):
                if what == "S":
                    if n % GROUP == 0:
                        pe.wait_ge(packed[n // GROUP], g * 128 + 128)
                    for t in range(TILES):
                        u = S_use(n, t)
                        wait_S_bank(pe, g, u)
                        nc.tensor.matmul(S_bank[u % 2][:, :], q_pack[0:ONE_ROW + 1, n, t * P:(t + 1) * P],
                                         k_pack[0:ONE_ROW + 1, n, :], start=True, stop=True).then_inc(scored, 1)
                if what == "M":
                    u = 17 * n + 16
                    pe.wait_ge(maxed, g * 32 + 16 * (n + 1))
                    if n == 1:
                        wait_S_bank(pe, g, u)
                    nc.tensor.transpose(S_bank[u % 2][0:GROUP * TILES, 0:P], maxima[:, n * 16:(n + 1) * 16],
                                        ident).then_inc(max_turned, 1)
                if what == "T":
                    grp, kt = divmod(n, TILES)
                    if kt == 0:
                        pe.wait_ge(shift_packed, g * 32 + 16 * (grp + 1))
                    for j in range(GROUP):
                        u = n * GROUP + j
                        if not (first(g) and u < 2):
                            pe.wait_ge(barred_out, g * 32 + (u - 1))
                        h = grp * GROUP + j
                        nc.tensor.matmul(T_bank[u % 2][:, :], k_pack[:, h, kt * P:(kt + 1) * P], q_pack[:, h, :],
                                         start=True, stop=True).then_inc(shifted, 1)
                if what == "V":
                    grp, kt = divmod(n, TILES)
                    if n == 0:
                        pe.wait_ge(v_ready, g + 1)
                    if kt == 0 and not (first(g) and grp == 0):
                        pe.wait_ge(ctx_copied, g * 2 + grp)
                    pe.wait_ge(exped, g * 16 + 2 * (n + 1))
                    for j in range(GROUP):
                        last = nc.tensor.matmul(C_bank[j * SLOT:(j + 1) * SLOT, :],
                                                values[p][:, kt, grp * GROUP + j, :], probs[n % 4][:, j, :],
                                                start=(kt == 0), stop=(kt == TILES - 1),
                                                tile_position=(0, j * SLOT))
                    last.then_inc(weighted, 1)

            def turn(dst, src):
                for t in range(TILES):
                    last = nc.tensor.transpose(dst[:, t * P:(t + 1) * P], src[:, t, :], ident)
                return last

            def apply_w(dst, srcT, wt):
                for t in range(TILES):
                    last = nc.tensor.matmul(nat(dst)[:, t, :], srcT[:, t * P:(t + 1) * P], wt, start=True, stop=True)
                return last

            def later(what, n, g, p):
                if what == "turn_ctx":
                    pe.wait_ge(ctx_copied, g * 2 + 2)
                    if not first(g):
                        pe.wait_ge(pre_ready, g * 2)
                        pe.wait_ge(near_in, g * 2)
                    for t in range(TILES):
                        for grp in range(GROUPS):
                            c = (t % 2) * 256 + grp * P
                            last = nc.tensor.transpose(X_pair[:, t // 2, c:c + P], ctx_T[grp][:, t * P:(t + 1) * P], ident)
                    last.then_inc(ctx_turned, 1)
                if what == "wo":
                    pe.wait_ge(ctx_scaled, g + 1)
                    if not first(g):
                        pe.wait_ge(root_in, g * 2)
                    else:
                        pe.wait_ge(v_ready, 2)
                    turn(X[2], ctx_nat).then_inc(ctx_back, 1)
                    pe.wait_ge(ctx_back_in, g + 1)
                    apply_w(X[0], turned_a, w("o")).then_inc(wo_done, 1)
                if what == "turn_z":
                    pe.wait_ge(normed, g * 6 + 1)
                    turn(X[1], n_d).then_inc(z_turned, 1)
                if what == "ff1":
                    pe.wait_ge(z_in, g + 1)
                    for f, b in enumerate((2, 0, 1, 2)):
                        if f == 3:
                            pe.wait_ge(ff1_in, g * 4 + 1)
                        nc.tensor.matmul(X[b], w("ff1", f * P, (f + 1) * P), turned_b[:, :],
                                         start=True, stop=True).then_inc(ff1_done, 1)
                if what == "ff2":
                    pe.wait_ge(ff1_in, g * 4 + 4)
                    for t in range(TILES):
                        for f in range(FT):
                            last = nc.tensor.matmul(nat(X[0])[:, t, :], big_a[:, f, t * P:(t + 1) * P],
                                                    w("ff2", f * P, (f + 1) * P), start=(f == 0), stop=(f == FT - 1))
                    last.then_inc(ff2_done, 1)
                if what == "turn_y1":
                    pe.wait_ge(normed, g * 6 + 3)
                    turn(X[1], n_a).then_inc(y1_turned, 1)
                if what == "gat_in":
                    pe.wait_ge(y1_in, g + 1)
                    nc.tensor.matmul(X[2], gat_right[:, :], turned_a[:, :], start=True,
                                     stop=True).then_inc(gat_right_done, 1)
                    for t in range(TILES):
                        c = (t % 2) * 256
                        last = nc.tensor.matmul(X_pair[:, t // 2, c:c + DIM + 1], turned_a[:, t * P:(t + 1) * P],
                                                gat_ext[:, :], start=True, stop=True)
                    last.then_inc(h_done, 1)
                if what == "gat_turn":
                    pe.wait_ge(gat_exped, g * 4 + 4)
                    for jt, b in enumerate((0, 1, 2, 0)):
                        if jt == 0:
                            pe.wait_ge(h_in, g + 1)
                        if jt == 3:
                            pe.wait_ge(gat_pT_in, g * 4 + 1)
                        for it in range(TILES):
                            last = nc.tensor.transpose(X[b][:, it * P:(it + 1) * P],
                                                       big_b[:, it, jt * P:(jt + 1) * P], ident)
                        last.then_inc(gat_pT, 1)
                if what == "gat_sum":
                    pe.wait_ge(gat_pT_in, g * 4 + 4)
                    for it in range(TILES):
                        for jt in range(TILES):
                            last = nc.tensor.matmul(nat(X[1])[:, it, :], big_a[:, jt, it * P:(it + 1) * P],
                                                    h_ext[:, jt, 0:DIM], start=(jt == 0), stop=(jt == TILES - 1))
                    last.then_inc(gat_done, 1)
                if what == "agg":
                    if n == 0:
                        pe.wait_ge(lo_ready, g * 2 + 1)
                        pe.wait_ge(hi_ready, g * 2 + 1)
                    for r in (2 * n, 2 * n + 1):
                        pe.wait_ge(rel_mask, g * 4 + r + 1)
                        if r == 3:
                            pe.wait_ge(agg_in, g * 4 + 1)
                        dst = X[(2, 0, 1, 2)[r]]
                        for mt in range(TILES):
                            for k, part in enumerate((part_hi, part_lo)):
                                last = nc.tensor.matmul(dst, part[:, mt, :], is_rel[r % 2][:, mt, :],
                                                        start=(mt == 0 and k == 0), stop=(mt == TILES - 1 and k == 1))
                        last.then_inc(agg_done, 1)
                if what == "rel":
                    pe.wait_ge(agg_in, g * 4 + 4)
                    if not (isinstance(g, int) and g >= GRAPHS - 2):
                        pe.wait_ge(qk_lo, g * 2 + 5)
                    for t in range(TILES):
                        for r in range(RELS):
                            last = nc.tensor.matmul(nat(X[0])[:, t, :], big_b[:, r, t * P:(t + 1) * P],
                                                    w("rel", r * P, (r + 1) * P), start=(r == 0), stop=(r == RELS - 1))
                    last.then_inc(rel_done, 1)
                if what == "near1":
                    pe.wait_ge(normed, g * 6 + 5)
                    turn(X[1], n_d).then_inc(y3_turned, 1)
                    pe.wait_ge(lo_ready, g * 2 + 2)
                    pe.wait_ge(hi_ready, g * 2 + 2)
                    pe.wait_ge(one_mask, g + 1)
                    for it in range(TILES):
                        for k, part in enumerate((part_hi, part_lo)):
                            last = nc.tensor.matmul(X[2], part[:, it, :], is_one[:, it, :],
                                                    start=(it == 0 and k == 0), stop=(it == TILES - 1 and k == 1))
                    last.then_inc(near_done, 1)
                    for jt in range(TILES):
                        for it in range(TILES):
                            last = nc.tensor.matmul(X[0][:, 2 * jt:2 * jt + 2], is_one[:, it, jt * P:(jt + 1) * P],
                                                    ones16[:, :], start=(it == 0), stop=(it == TILES - 1))
                    last.then_inc(deg_done, 1)
                if what in ("conv1", "conv2"):
                    c = 0 if what == "conv1" else 1
                    rootT, root_w, near_w = ((turned_b, "root1", "near1"), (turned_a, "root2", "near2"))[c]
                    nearT = (turned_a, turned_b)[c]
                    banks = ((1, 2), (2, 0))[c]
                    pe.wait_ge(y3_in if c == 0 else h1_in, g + 1)
                    if c == 1:
                        pe.wait_ge(pre_ready, g * 2 + 1)
                    apply_w(X[banks[0]], rootT, w(root_w)).then_inc(root_done, 1)
                    pe.wait_ge(near_in, g * 2 + c + 1)
                    apply_w(X[banks[1]], nearT, w(near_w)).then_inc(near_w_done, 1)
                if what == "near2":
                    pe.wait_ge(elu_ready, g * 2 + 1)
                    pe.wait_ge(deg_ready, g + 1)
                    turn(X[0], n_f).then_inc(h1_turned, 1)
                    pe.wait_ge(part3, g + 1)
                    pe.wait_ge(part2, g + 1)
                    for it in range(TILES):
                        for k, part in enumerate(h_parts):
                            last = nc.tensor.matmul(X[1], part[:, it, :], is_one[:, it, :],
                                                    start=(it == 0 and k == 0), stop=(it == TILES - 1 and k == 2))
                    last.then_inc(near_done, 1)

            def step(i, p, tail, attn, proj):
                for what, n in ORDER:
                    if what in "SMTV" and attn is not None:
                        attention(what, n, attn, p)
                    elif what == "proj" and proj is not None:
                        project(proj)
                    elif tail is not None:
                        later(what, n, tail, 1 - p)

            steps(pe, step)

        @block.scalar
        def _(act):
            act.wait_ge(weights_in, 48)
            act.wait_ge(gat_w_psum, 1)
            nc.scalar.activation(gat_right[:, :], X[1][:, 0:P], ACT.Copy)
            nc.scalar.activation(gat_ext[:, 0:DIM], w("gat"), ACT.Copy)
            nc.scalar.activation(gat_ext[:, DIM:DIM + 1], X[1][:, P:P + 1], ACT.Copy).then_inc(gat_w_ready, 1)

            def project(g):
                if not first(g):
                    act.wait_ge(bounced, g * 64)
                for n, (dst, b, bias) in enumerate(((q_hi, 0, "bq"), (k_hi, 1, "bk"))):
                    act.wait_ge(qk_proj, g * 2 + (n + 1))
                    nc.scalar.activation(dst[:, :], X[b], ACT.Identity, bias=col(bias)).then_inc(qk_hi, 1)

            project(0)

            def attention(what, n, g, p):
                if what == "M":
                    act.wait_ge(max_turned, g * 2 + (n + 1))
                    if not (first(g) and n == 0):
                        act.wait_ge(shift_packed, g * 32 + 16 * n)
                    u = 17 * n + 16
                    nc.scalar.activation(shift[:, :], S_bank[u % 2][0:GROUP * TILES, 0:P], ACT.Copy,
                                         scale=-1.0).then_inc(shift_ready, 1)
                if what == "T":
                    for j in range(2):
                        act.wait_ge(barred_out, g * 32 + n * 4 + 2 * (j + 1))
                        s = probs[n % 4][:, 2 * j:2 * j + 2, :]
                        nc.scalar.activation(s, s, ACT.Exp, scale=SCALE).then_inc(exped, 1)
                if what == "C":
                    act.wait_ge(weighted, g * 8 + 4 * (n + 1))
                    if not first(g):
                        act.wait_ge(ctx_turned, g)
                    nc.scalar.activation(ctx_T[n][:, :], C_bank[:, :], ACT.Copy).then_inc(ctx_copied, 1)

            def later(what, n, g, p):
                if what == "wo":
                    act.wait_ge(ctx_back, g + 1)
                    nc.scalar.activation(turned_a[:, :], X[2], ACT.Copy).then_inc(ctx_back_in, 1)
                if what == "turn_z":
                    act.wait_ge(z_turned, g + 1)
                    nc.scalar.activation(turned_b[:, :], X[1], ACT.Identity, bias=col("b1"),
                                         scale=col("g1")).then_inc(z_in, 1)
                if what == "ff1":
                    for f, b in enumerate((2, 0, 1, 2)):
                        act.wait_ge(ff1_done, g * 4 + f + 1)
                        nc.scalar.activation(big_a[:, f, :], X[b], ACT.Relu, bias=col(f"ff1_{f}")).then_inc(ff1_in, 1)
                if what == "turn_y1":
                    act.wait_ge(y1_turned, g + 1)
                    nc.scalar.activation(turned_a[:, :], X[1], ACT.Copy).then_inc(y1_in, 1)
                if what == "gat_in":
                    act.wait_ge(h_done, g + 1)
                    for b in range(2):
                        last = nc.scalar.activation(h_ext[:, 2 * b:2 * b + 2, :],
                                                    X[b].rearrange("p (t c) -> p t c", t=2)[:, :, 0:DIM + 1], ACT.Copy)
                    last.then_inc(h_in, 1)
                if what == "gat_exp":
                    act.wait_ge(gat_leaky, g + 1)
                    act.wait_ge(gat_low_ready, g + 1)
                    for t in range(TILES):
                        nc.scalar.activation(big_b[:, t, :], big_b[:, t, :], ACT.Exp, bias=gat_low[:, t:t + 1],
                                             accum_out=gat_total[:, t:t + 1]).then_inc(gat_exped, 1)
                if what == "gat_turn":
                    for jt, b in enumerate((0, 1, 2, 0)):
                        act.wait_ge(gat_pT, g * 4 + jt + 1)
                        nc.scalar.activation(big_a[:, jt, :], X[b], ACT.Copy).then_inc(gat_pT_in, 1)
                if what in ("gat_sum", "rel"):
                    c, y = (0, n_b) if what == "gat_sum" else (1, n_d)
                    act.wait_ge(normed, g * 6 + 4 + c)
                    nc.scalar.activation(part_hi[:, :, :], y[:, :, :], ACT.Copy, scale=UP).then_inc(hi_ready, 1)
                if what == "agg":
                    for r in (2 * n, 2 * n + 1):
                        act.wait_ge(agg_done, g * 4 + r + 1)
                        nc.scalar.activation(big_b[:, r, :], X[(2, 0, 1, 2)[r]], ACT.Copy,
                                             scale=1.0 / UP).then_inc(agg_in, 1)
                if what == "near1":
                    act.wait_ge(y3_turned, g + 1)
                    nc.scalar.activation(turned_b[:, :], X[1], ACT.Copy).then_inc(y3_in, 1)
                    act.wait_ge(near_done, g * 2 + 1)
                    nc.scalar.activation(turned_a[:, :], X[2], ACT.Copy, scale=1.0 / UP).then_inc(near_in, 1)
                if what in ("conv1", "conv2"):
                    c = 0 if what == "conv1" else 1
                    act.wait_ge(pre_low, g * 2 + c + 1)
                    nc.scalar.activation(n_f[:, :, :], n_f[:, :, :], ACT.Exp).then_inc(pre_exp, 1)
                    if c == 0:
                        act.wait_ge(elu_ready, g * 2 + 1)
                        nc.scalar.activation(h_parts[0][:, :, :], n_f[:, :, :], ACT.Copy).then_inc(part1, 1)
                        act.wait_ge(rest1, g + 1)
                        nc.scalar.activation(h_parts[1][:, :, :], n_c[:, :, :], ACT.Copy).then_inc(part2, 1)
                if what == "near2":
                    act.wait_ge(h1_turned, g + 1)
                    nc.scalar.activation(turned_a[:, :], X[0], ACT.Copy).then_inc(h1_in, 1)
                    act.wait_ge(near_done, g * 2 + 2)
                    nc.scalar.activation(turned_b[:, :], X[1], ACT.Copy).then_inc(near_in, 1)

            def step(i, p, tail, attn, proj):
                for what, n in ORDER:
                    if what in "SMTVC" and attn is not None:
                        attention(what, n, attn, p)
                    elif what == "proj" and proj is not None:
                        project(proj)
                    elif tail is not None:
                        later(what, n, tail, 1 - p)
                        if what == "gat_in":
                            later("gat_exp", n, tail, 1 - p)

            steps(act, step)

        @block.vector
        def _(dve):
            for p in range(2):
                nc.vector.memset(values[p][:, :, :, :], 0.0).then_inc(values_zeroed, 1)
            dve.wait_ge(values_zeroed, 2)
            for p in range(2):
                nc.vector.memset(values[p][:, :, :, HEAD:HEAD + 1], 1.0)
            nc.vector.memset(q_pack[PACK:SHIFT_ROW + 1, :, :].bitcast(F32), 0.0)
            nc.vector.memset(k_pack[PACK:SHIFT_ROW + 1, :, :].bitcast(F32), 1.0)
            nc.vector.memset(ones16[:, :], 1.0).then_inc(dve_consts, 1)
            dve.wait_ge(weights_in, 48)
            nc.vector.tensor_copy(a_right[:, :], col("a_r").broadcast_to((P, P))).then_inc(gat_a_ready, 1)
            nc.vector.tensor_scalar(not_self[:, :], w("ident"), -1.0, 1.0, ALU.mult, ALU.add).then_inc(dve_consts, 1)
            dve.wait_ge(dve_consts, 2)

            def prep(g, p, n):
                if n == 0:
                    dve.wait_ge(adj_in_sem, g * 32 + 32)
                    if not (isinstance(g, int) and g < 2):
                        dve.wait_ge(rel_mask, g * 4 - 4)
                    nc.vector.tensor_scalar(codes[p][:, :, :], adj_in[:, :, :], 0.0, RELS + 1.0, ALU.max,
                                            ALU.min).then_inc(coded, 1)
                    nc.vector.tensor_scalar(codesT[p][:, :, :], adjT_in[:, :, :], 0.0, RELS + 1.0, ALU.max,
                                            ALU.min).then_inc(coded, 1)
                else:
                    dve.wait_ge(coded, g * 2 + 2)
                    nc.vector.tensor_tensor(barred[p][:, :, :], codes[p][:, :, :], codesT[p][:, :, :],
                                            ALU.max).then_inc(allow, 1)
                    dve.wait_ge(allow, g * 3 + 1)
                    nc.vector.tensor_scalar(barred[p][:, :, :], barred[p][:, :, :], 0.5, NEVER, ALU.is_lt,
                                            ALU.mult).then_inc(allow, 1)
                    dve.wait_ge(allow, g * 3 + 2)
                    for t in range(TILES):
                        d = barred[p][:, t, t * P:(t + 1) * P]
                        last = nc.vector.tensor_tensor(d, d, not_self[:, :], ALU.mult)
                    last.then_inc(allow, 1)

            def project(g, p):
                for n, (dst, hi, b, bias) in enumerate(((q_lo, q_hi, 0, "bq"), (k_lo, k_hi, 1, "bk"))):
                    dve.wait_ge(qk_hi, g * 2 + (n + 1))
                    if n == 0 and not first(g):
                        dve.wait_ge(bounced, g * 64)
                    nc.vector.scalar_tensor_tensor(dst[:, :], X[b], col(bias), hi[:, :].bitcast(F32), ALU.add,
                                                   ALU.subtract).then_inc(qk_lo, 1)
                dve.wait_ge(v_proj, g + 1)
                nc.vector.tensor_tensor(
                    values[p][:, :, :, 0:HEAD], X[2].rearrange("p (t h d) -> p t h d", t=TILES, h=HEADS),
                    rows[:, 0:1, :].rearrange("p o (h d) -> p o h d", h=HEADS).broadcast_to((P, TILES, HEADS, HEAD)),
                    ALU.add).then_inc(v_ready, 1)

            prep(0, 0, 0)
            prep(0, 0, 1)
            project(0, 0)

            def attention(what, n, g, p):
                if what == "S":
                    if n == 0:
                        dve.wait_ge(allow, g * 3 + 3)
                    for t in range(TILES):
                        alone(dve, scored, g * 32 + n * TILES + t + 1)
                        u = S_use(n, t)
                        nc.vector.tensor_tensor_reduce(
                            out=S_bank[u % 2][:, :], in0=S_bank[u % 2][:, :], in1=barred[p][:, t, :], scale=1.0,
                            scalar=-3e38, op0=ALU.add, op1=ALU.max,
                            accum_out=maxima[:, n * TILES + t:n * TILES + t + 1]).then_inc(maxed, 1)
                if what == "T":
                    kt = n % TILES
                    if not (first(g) and n < 4):
                        dve.wait_ge(weighted, g * 8 + (n - 3))
                    for j in range(GROUP):
                        u = n * GROUP + j
                        dve.wait_ge(shifted, g * 32 + (u + 1))
                        nc.vector.tensor_tensor(probs[n % 4][:, j, :], T_bank[u % 2][:, :], barred[p][:, kt, :],
                                                ALU.add).then_inc(barred_out, 1)

            def normalise(g, k, src, dst):
                dve.wait_ge(resid_ready, g * 6 + k + 1)
                for t in range(TILES):
                    last = nc.vector.bn_stats(stats[:, t, :], src[:, t, :])
                last.then_inc(stats_ready, 1)
                alone(dve, stats_ready, g * 6 + k + 1)
                for t in range(TILES):
                    last = nc.vector.bn_aggr(moments[:, t, :], stats[:, t, :])
                last.then_inc(moments_ready, 1)
                dve.wait_ge(rstd_ready, g * 6 + k + 1)
                for t in range(TILES):
                    last = nc.vector.tensor_scalar(dst[:, t, :], src[:, t, :], moments[:, t, 0:1], rstd[:, t:t + 1],
                                                   ALU.subtract, ALU.mult)
                last.then_inc(normed, 1)

            def split_low(g, c, y):
                dve.wait_ge(hi_ready, g * 2 + c + 1)
                nc.vector.scalar_tensor_tensor(part_lo[:, :, :], y[:, :, :], UP, part_hi[:, :, :], ALU.mult,
                                               ALU.subtract).then_inc(lo_ready, 1)

            def later(what, n, g, p):
                if what == "early":
                    nc.vector.tensor_scalar(no_edge[:, :, :], codes[p][:, :, :], 0.5, NEG_BIG / ALPHA, ALU.is_lt,
                                            ALU.mult).then_inc(no_edge_ready, 1)
                if what == "unit":
                    nc.vector.tensor_scalar(is_one[:, :, :], codes[p][:, :, :], 1.0, None,
                                            ALU.is_equal).then_inc(one_mask, 1)
                if what == "turn_ctx":
                    dve.wait_ge(ctx_turned, g + 1)
                    src = X_pair[:, :, :].rearrange("p b (s d) -> p (b s) d", d=SLOT)
                    nc.vector.reciprocal(ctx_sum[:, :].rearrange("p (s o) -> p s o", o=1),
                                         src[:, :, HEAD:HEAD + 1]).then_inc(ctx_inv, 1)
                    dve.wait_ge(ctx_inv, g + 1)
                    nc.vector.tensor_tensor(
                        ctx_nat[:, :, :].rearrange("p t (h d) -> p (t h) d", h=HEADS), src[:, :, 0:HEAD],
                        ctx_sum[:, :].rearrange("p (s o) -> p s o", o=1).broadcast_to((P, TILES * HEADS, HEAD)),
                        ALU.mult).then_inc(ctx_scaled, 1)
                if what == "wo":
                    dve.wait_ge(wo_done, g + 1)
                    dve.wait_ge(x_bo, g + 1)
                    nc.vector.tensor_tensor(resid[:, :, :], nat(X[0]), n_a[:, :, :], ALU.add).then_inc(resid_ready, 1)
                    normalise(g, 0, resid, n_d)
                if what == "ff2":
                    dve.wait_ge(ff2_done, g + 1)
                    dve.wait_ge(x1_ready, g + 1)
                    nc.vector.tensor_tensor(resid[:, :, :], nat(X[0]), n_b[:, :, :], ALU.add).then_inc(resid_ready, 1)
                    normalise(g, 1, resid, n_e)
                    normalise(g, 2, resid, n_a)
                if what == "gat_in":
                    dve.wait_ge(gat_right_done, g + 1)
                    alone(dve, no_edge_ready, g + 1)
                    for t in range(TILES):
                        last = nc.vector.tensor_tensor_reduce(
                            out=big_b[:, t, :], in0=X[2], in1=no_edge[:, t, :], scale=1.0, scalar=-3e38,
                            op0=ALU.add, op1=ALU.max, accum_out=gat_max[:, t:t + 1])
                        last.then_inc(gat_maxed, 1)
                    dve.wait_ge(gat_maxed, g * 4 + 4)
                    dve.wait_ge(h_in, g + 1)
                    own = h_ext[:, :, DIM:DIM + 1]
                    nc.vector.tensor_tensor(gat_max[:, :].rearrange("p (t o) -> p t o", o=1),
                                            gat_max[:, :].rearrange("p (t o) -> p t o", o=1), own,
                                            ALU.add).then_inc(gat_sum_max, 1)
                    for t in range(TILES):
                        last = nc.vector.tensor_scalar(big_b[:, t, :], big_b[:, t, :], h_ext[:, t, DIM:DIM + 1], None,
                                                       ALU.add)
                    last.then_inc(gat_e, 1)
                    dve.wait_ge(gat_sum_max, g + 1)
                    nc.vector.scalar_tensor_tensor(gat_top[:, :], gat_max[:, :], ALPHA, gat_max[:, :], ALU.mult,
                                                   ALU.max).then_inc(gat_top_ready, 1)
                    dve.wait_ge(gat_e, g + 1)
                    nc.vector.scalar_tensor_tensor(big_b[:, :, :], big_b[:, :, :], ALPHA, big_b[:, :, :], ALU.mult,
                                                   ALU.max).then_inc(gat_leaky, 1)
                    dve.wait_ge(gat_top_ready, g + 1)
                    nc.vector.tensor_scalar(gat_low[:, :], gat_top[:, :], -1.0, None,
                                            ALU.mult).then_inc(gat_low_ready, 1)
                if what == "gat_sum":
                    dve.wait_ge(gat_exped, g * 4 + 4)
                    nc.vector.reciprocal(gat_inv[:, :], gat_total[:, :]).then_inc(gat_inv_ready, 1)
                    dve.wait_ge(gat_inv_ready, g + 1)
                    dve.wait_ge(gat_done, g + 1)
                    for t in range(TILES):
                        last = nc.vector.scalar_tensor_tensor(resid[:, t, :], nat(X[1])[:, t, :], gat_inv[:, t:t + 1],
                                                              n_a[:, t, :], ALU.mult, ALU.add)
                    last.then_inc(resid_ready, 1)
                    normalise(g, 3, resid, n_b)
                    split_low(g, 0, n_b)
                if what == "agg":
                    for r in (2 * n, 2 * n + 1):
                        if r >= 2:
                            dve.wait_ge(agg_done, g * 4 + r - 1)
                        elif not first(g):
                            dve.wait_ge(agg_done, g * 4 + r - 1)
                        nc.vector.tensor_scalar(is_rel[r % 2][:, :, :], codesT[p][:, :, :], r + 1.0, None,
                                                ALU.is_equal).then_inc(rel_mask, 1)
                if what == "rel":
                    dve.wait_ge(rel_done, g + 1)
                    dve.wait_ge(y2_bias, g + 1)
                    nc.vector.tensor_tensor(resid[:, :, :], nat(X[0]), n_c[:, :, :], ALU.add).then_inc(resid_ready, 1)
                    normalise(g, 4, resid, n_d)
                    split_low(g, 1, n_d)
                if what == "near1":
                    dve.wait_ge(deg_done, g + 1)
                    nc.vector.tensor_scalar(degree[:, :].rearrange("p (t o) -> p t o", o=1),
                                            X[0][:, 0:2 * TILES].rearrange("p (t o) -> p t o", o=2)[:, :, 0:1],
                                            1.0, None, ALU.max).then_inc(deg_ready, 1)
                    dve.wait_ge(deg_ready, g + 1)
                    nc.vector.reciprocal(deg_inv[:, :], degree[:, :]).then_inc(deg_inv_ready, 1)
                if what in ("conv1", "conv2"):
                    c = 0 if what == "conv1" else 1
                    b_root, b_near = ((1, 2), (2, 0))[c]
                    dve.wait_ge(root_done, g * 2 + c + 1)
                    nc.vector.tensor_tensor(n_e[:, :, :], nat(X[b_root]), row4("c1" if c == 0 else "c2"),
                                            ALU.add).then_inc(root_in, 1)
                    dve.wait_ge(near_w_done, g * 2 + c + 1)
                    dve.wait_ge(root_in, g * 2 + c + 1)
                    dve.wait_ge(deg_inv_ready, g + 1)
                    for t in range(TILES):
                        last = nc.vector.scalar_tensor_tensor(n_e[:, t, :], nat(X[b_near])[:, t, :],
                                                              deg_inv[:, t:t + 1], n_e[:, t, :], ALU.mult, ALU.add)
                    last.then_inc(pre_ready, 1)
                    dve.wait_ge(pre_ready, g * 2 + c + 1)
                    nc.vector.tensor_scalar(n_f[:, :, :], n_e[:, :, :], 0.0, None, ALU.min).then_inc(pre_low, 1)
                    dve.wait_ge(pre_exp, g * 2 + c + 1)
                    nc.vector.scalar_tensor_tensor(n_f[:, :, :], n_f[:, :, :], -1.0, n_e[:, :, :], ALU.add,
                                                   ALU.max).then_inc(elu_ready, 1)
                    if c == 0:
                        dve.wait_ge(part1, g + 1)
                        nc.vector.tensor_tensor(n_c[:, :, :], n_f[:, :, :], h_parts[0][:, :, :],
                                                ALU.subtract).then_inc(rest1, 1)
                        dve.wait_ge(part2, g + 1)
                        nc.vector.tensor_tensor(h_parts[2][:, :, :], n_c[:, :, :], h_parts[1][:, :, :],
                                                ALU.subtract).then_inc(part3, 1)
                    else:
                        dve.wait_ge(elu_ready, g * 2 + 2)
                        nc.vector.tensor_tensor(resid[:, :, :], n_f[:, :, :], n_d[:, :, :],
                                                ALU.add).then_inc(resid_ready, 1)
                        if not first(g):
                            dve.wait_ge(stored, g * 16)
                        normalise(g, 5, resid, result)

            def step(i, p, tail, attn, proj):
                for what, n in ORDER:
                    if what in "SMTVC":
                        if attn is not None:
                            attention(what, n, attn, p)
                    elif what == "prep":
                        if proj is not None:
                            prep(proj, 1 - p, n)
                    elif what == "proj":
                        if proj is not None:
                            project(proj, 1 - p)
                    elif tail is not None:
                        later(what, n, tail, 1 - p)

            steps(dve, step)

        @block.gpsimd
        def _(pool):
            nc.gpsimd.memset(eps_tile[:, :], EPS).then_inc(pool_consts, 1)
            nc.gpsimd.memset(half_tile[:, :], -0.5).then_inc(pool_consts, 1)
            pool.wait_ge(weights_in, 48)
            pool.wait_ge(pool_consts, 2)
            nc.gpsimd.tensor_tensor(ff_bias[:, :], rows[:, ROWS.index("b1"), :], rows[:, ROWS.index("ff2"), :],
                                    ALU.add).then_inc(ff_bias_ready, 1)
            pool.wait_ge(ff_bias_ready, 1)

            def root_of(g, k):
                pool.wait_ge(moments_ready, g * 6 + k + 1)
                nc.gpsimd.tensor_tensor(spread[:, :].rearrange("p (t o) -> p t o", o=1), moments[:, :, 1:2],
                                        eps_tile[:, :].rearrange("p (t o) -> p t o", o=1),
                                        ALU.add).then_inc(spread_ready, 1)
                pool.wait_ge(spread_ready, g * 6 + k + 1)
                nc.gpsimd.tensor_tensor(rstd[:, :], spread[:, :], half_tile[:, :], ALU.pow).then_inc(rstd_ready, 1)

            def later(what, n, g, p):
                if what == "early":
                    pool.wait_ge(x_in, g * 16 + 16)
                    if not first(g):
                        pool.wait_ge(resid_ready, g * 6)
                    nc.gpsimd.tensor_tensor(n_a[:, :, :], x_nat[:, :, :], row4("bo"), ALU.add).then_inc(x_bo, 1)
                    nc.gpsimd.tensor_tensor(n_c[:, :, :], x_nat[:, :, :], row4("b2"), ALU.add).then_inc(x_b2, 1)
                if what == "wo":
                    root_of(g, 0)
                if what == "turn_z":
                    pool.wait_ge(normed, g * 6 + 1)
                    nc.gpsimd.tensor_tensor(n_b[:, :, :], n_d[:, :, :], row4("g1"), ALU.mult).then_inc(z_scaled, 1)
                    pool.wait_ge(z_scaled, g + 1)
                    nc.gpsimd.tensor_tensor(n_b[:, :, :], n_b[:, :, :],
                                            ff_bias[:, :].rearrange("p (o c) -> p o c", o=1)
                                            .broadcast_to((P, TILES, DIM)), ALU.add).then_inc(x1_ready, 1)
                if what == "ff2":
                    root_of(g, 1)
                    pool.wait_ge(normed, g * 6 + 2)
                    nc.gpsimd.tensor_tensor(n_e[:, :, :], n_e[:, :, :], row4("g2"), ALU.mult).then_inc(z2_scaled, 1)
                    pool.wait_ge(z2_scaled, g + 1)
                    nc.gpsimd.tensor_tensor(resid[:, :, :], n_e[:, :, :], n_c[:, :, :], ALU.add).then_inc(resid_ready, 1)
                    root_of(g, 2)
                if what == "gat_sum":
                    root_of(g, 3)
                    pool.wait_ge(normed, g * 6 + 4)
                    nc.gpsimd.tensor_tensor(n_c[:, :, :], n_b[:, :, :], row4("bias"), ALU.add).then_inc(y2_bias, 1)
                if what == "rel":
                    root_of(g, 4)
                if what == "conv2":
                    root_of(g, 5)

            def step(i, p, tail, attn, proj):
                for what, n in ORDER:
                    if tail is not None:
                        later(what, n, tail, 1 - p)

            steps(pool, step)


_INPUTS = ("x", "xT", "adj", "adjT", "weights", "vec_rows", "vec_cols")


def kernel(**inputs):
    import numpy as np
    import concourse.bacc as bacc
    from concourse.bass_utils import run_bass_kernel_spmd

    a = {k: np.asarray(v) for k, v in inputs.items()}
    lay = np.ascontiguousarray
    f32 = np.float32

    def tiled(m):
        return lay(m.reshape(GRAPHS, TILES, P, m.shape[2]).transpose(0, 2, 1, 3)).reshape(GRAPHS, P, -1)

    wqkv = a["L0_gnn_Wqkv"]
    pieces = {
        "q": wqkv[0:DIM].T, "k": wqkv[DIM:2 * DIM].T, "v": wqkv[2 * DIM:].T, "o": a["L0_gnn_Wo"].T,
        "ff1": a["L0_gnn_W1"].T,
        "ff2": a["L0_gnn_W2"].T.reshape(FT, P, DIM).transpose(1, 0, 2).reshape(P, FT * DIM),
        "gat": a["L1_gnn_W"], "gatT": a["L1_gnn_W"].T,
        "rel": a["L2_gnn_weight"].transpose(1, 0, 2).reshape(P, RELS * DIM),
        "root1": a["L3_gnn_w_root1"], "near1": a["L3_gnn_w_rel1"][1],
        "root2": a["L3_gnn_w_root2"], "near2": a["L3_gnn_w_rel2"][1],
        "ident": np.eye(P, dtype=f32),
    }
    bqkv = a["L0_gnn_bqkv"]
    vec = {
        "bq": bqkv[0:DIM], "bk": bqkv[DIM:2 * DIM], "bv": bqkv[2 * DIM:], "bo": a["L0_gnn_bo"],
        "g1": a["L0_gnn_ln1_g"], "b1": a["L0_gnn_ln1_b"], "g2": a["L0_gnn_ln2_g"], "b2": a["L0_gnn_ln2_b"],
        "ff2": a["L0_gnn_b2"], "bias": a["L2_gnn_bias"], "c1": a["L3_gnn_b1"], "c2": a["L3_gnn_b2"],
        "a_l": a["L1_gnn_a"][0:DIM, 0], "a_r": a["L1_gnn_a"][DIM:, 0],
    }
    for f in range(FT):
        vec[f"ff1_{f}"] = a["L0_gnn_b1"][f * P:(f + 1) * P]
    arrays = {
        "x": tiled(a["x"]), "xT": lay(a["x"].transpose(0, 2, 1)),
        "adj": tiled(a["adj"]), "adjT": tiled(a["adj"].transpose(0, 2, 1)),
        "weights": lay(np.concatenate([pieces[n] for n in W_COLS], axis=1)),
        "vec_rows": lay(np.concatenate([vec[n] for n in ROWS])),
        "vec_cols": lay(np.stack([vec[n] for n in VECS], axis=1)),
    }
    nc = bacc.Bacc("TRN2", target_bir_lowering=False, num_devices=1)
    args = [nc.dram_tensor(n, arrays[n].shape, mybir.dt.from_np(arrays[n].dtype), kind="ExternalInput").ap()
            for n in _INPUTS]
    out = nc.dram_tensor("out", (GRAPHS, P, TILES * DIM), F32, kind="ExternalOutput").ap()
    build(nc, *args, out)
    got = run_bass_kernel_spmd(nc, [arrays], core_ids=[0]).results[0]["out"]
    return got.reshape(GRAPHS, P, TILES, DIM).transpose(0, 2, 1, 3).reshape(GRAPHS, NODES, DIM)
```

```python
from contextlib import ExitStack

import concourse.bass as bass
from concourse import mybir

ALU = mybir.AluOpType
ACT = mybir.ActivationFunctionType
F32 = mybir.dt.float32
F32R = mybir.dt.float32r
F16 = mybir.dt.float16
BF16 = mybir.dt.bfloat16
I32 = mybir.dt.int32

GRAPHS, NODES, DIM = 16, 512, 128
P = 128
TILES = NODES // P
HEADS = 8
HEAD = DIM // HEADS
GROUP = 4
GROUPS = HEADS // GROUP
SLOT = 32
DFF = 4 * DIM
FT = DFF // P
RELS = 4
EPS = 1e-5
SCALE = 1.0 / HEAD ** 0.5
NEVER = -1e30
NEG_BIG = -9e15
ALPHA = 0.2
UP = 4096.0
PACK = 64
ONE_ROW, SHIFT_ROW = PACK, PACK + 1

W_COLS = {}
_at = 0
for _n, _w in (("q", P), ("k", P), ("v", P), ("o", P), ("ff1", DFF), ("ff2", DFF), ("gat", P), ("gatT", P),
               ("rel", RELS * P), ("root1", P), ("near1", P), ("root2", P), ("near2", P), ("ident", P)):
    W_COLS[_n] = (_at, _at + _w)
    _at += _w
W_ALL = _at

VECS = ("bq", "bk", "bv", "bo", "g1", "b1", "g2", "b2", "ff1_0", "ff1_1", "ff1_2", "ff1_3", "ff2", "bias", "c1", "c2",
        "a_l", "a_r")
ROWS = ("bv", "bo", "g1", "b1", "g2", "b2", "ff2", "bias", "c1", "c2")

SCORE_TILES = HEADS * TILES
HALF = SCORE_TILES // 2
S_BEAT = [n for n in range(HALF)] + [HALF + 2 * n for n in range(HALF)]
T_BEAT = [19 + 2 * n for n in range(HALF)] + [51 + n * 0.8 for n in range(HALF)]
SCORES = [(b, "attn", "S", n) for n, b in enumerate(S_BEAT)]
SHIFTED = [(b, "attn", "T", n) for n, b in enumerate(T_BEAT)]
MAXIMA = [(S_BEAT[HALF - 1] + 0.6, "attn", "M", 0), (S_BEAT[-1] + 0.6, "attn", "M", 1)]
SLOT_END = T_BEAT[GROUP - 1::GROUP]


def in_order(*tables):
    return sorted((e for t in tables for e in t), key=lambda e: e[0])


def spread_over(beat, per, role, what, count):
    return [(beat + per * n, role, what, n) for n in range(count)]


PE_TABLE = in_order(
    SCORES, SHIFTED, MAXIMA,
    [(SLOT_END[n] + 3.2, "attn", "V", n) for n in range(7)] + [(1.2, "mid", "V", 7)],
    [(4.2, "next", "proj", 0), (7.2, "next", "proj", 1), (10.2, "next", "proj", 2)],
    [(3.4, "mid", "turn_ctx", 0), (5.3, "mid", "turn_back", 0), (6.7, "mid", "wo", 0), (12.1, "mid", "turn_z", 0)],
    spread_over(13.3, 1.0, "mid", "ff1", FT), spread_over(18.3, 1.0, "mid", "ff2", TILES),
    [(32.1, "mid", "turn_y1", 0), (33.3, "mid", "gat_right", 0), (33.8, "mid", "gat_h", 0), (35.3, "mid", "gat_h", 1)],
    spread_over(44.3, 1.0, "mid", "gat_turn", TILES), spread_over(49.3, 1.0, "mid", "gat_sum", TILES),
    spread_over(0.4, 1.0, "late", "agg", 2 * RELS), [(2.6 + 2 * r, "late", "rel", r) for r in range(RELS)],
    [(14.6, "late", "turn_y3", 0), (16.6, "late", "near1", 0), (17.6, "late", "near1", 1), (18.6, "late", "degree", 0),
     (20.6, "late", "root", 0), (21.6, "late", "near_w", 0), (27.4, "late", "turn_h1", 0)],
    spread_over(30.4, 1.0, "late", "near2", 3),
    [(33.6, "late", "root", 1), (35.0, "late", "near_w", 1)],
)
ACT_TABLE = in_order(
    [(b + 0.4, "attn", "M", n) for b, _, _, n in MAXIMA], [(b + 0.5, "attn", "T", n) for n, b in enumerate(T_BEAT)],
    [(SLOT_END[3] + 4.0, "attn", "C", 0), (2.4, "mid", "C", 1)],
    [(4.8, "next", "proj", 0), (7.8, "next", "proj", 1)],
    [(6.3, "mid", "back", 0), (12.9, "mid", "z", 0)], spread_over(14.3, 1.0, "mid", "ff1", FT),
    [(32.9, "mid", "y1", 0), (34.8, "mid", "h", 0), (36.3, "mid", "h", 1)],
    spread_over(40.4, 1.0, "mid", "gat_exp", TILES), spread_over(45.2, 1.0, "mid", "gat_turn", TILES),
    [(58.2, "mid", "high", 0)],
    [(2.1 + 2 * r, "late", "agg", r) for r in range(RELS)],
    [(15.4, "late", "high", 0), (15.5, "late", "y3", 0), (18.5, "late", "near", 0), (24.2, "late", "elu", 0),
     (26.2, "late", "part", 0), (28.3, "late", "part", 1), (28.4, "late", "h1", 0), (33.4, "late", "near", 1),
     (37.4, "late", "elu", 1)],
)
NORM = ("stats", "moments", "apply")


def norm(beat, role, k):
    return [(beat, role, "stats", k), (beat + 1.0, role, "moments", k), (beat + 2.6, role, "apply", k)]


DVE_TABLE = in_order(
    SCORES,
    [(5.5, "next", "proj", 0), (8.5, "next", "proj", 1), (11.5, "next", "proj", 2)],
    [(4.3, "mid", "ctx", 0), (7.9, "mid", "resid", 0)], norm(8.2, "mid", 0),
    [(22.3, "mid", "resid", 1)], norm(22.6, "mid", 1), norm(28.6, "mid", 2),
    spread_over(34.4, 0.7, "mid", "gat_max", TILES), [(37.4, "mid", "gat_top", 0)],
    spread_over(37.6, 0.3, "mid", "gat_e", TILES), [(39.4, "mid", "leaky", 0)],
    [(46.4, "attn", "no_edge", 0), (48.6, "mid", "gat_inv", 0), (53.3, "mid", "resid", 3)], norm(53.6, "mid", 3),
    [(59.5, "mid", "low", 0)],
    [(50.4, "next", "codes", 0), (58.4, "next", "codes", 1), (61.4, "next", "barred", 0), (62.4, "next", "barred", 1),
     (62.9, "next", "barred", 2)],
    [(0.2, "late", "rel_mask", 0), (0.7, "late", "rel_mask", 1), (2.9, "late", "rel_mask", 2),
     (4.9, "late", "rel_mask", 3), (12.6, "late", "is_one", 0)],
    [(10.4, "late", "resid", 0)], norm(10.7, "late", 0),
    [(16.4, "late", "low", 0), (19.5, "late", "degree", 0)],
    [(21.5, "late", "root", 0), (22.6, "late", "pre", 0), (23.4, "late", "elu_low", 0), (25.3, "late", "elu", 0),
     (27.3, "late", "part", 0), (29.4, "late", "part", 1)],
    [(34.7, "late", "root", 1), (36.1, "late", "pre", 1), (36.6, "late", "elu_low", 1), (38.4, "late", "elu", 1),
     (39.6, "late", "resid", 1)], norm(40.6, "late", 1),
)
POOL_TABLE = in_order(
    [(0.0, "mid", "x", 0), (9.4, "mid", "rstd", 0), (12.0, "mid", "x1", 0), (23.8, "mid", "rstd", 1),
     (25.6, "mid", "y1", 0), (29.8, "mid", "rstd", 2), (54.8, "mid", "rstd", 3), (57.0, "mid", "y2", 0)],
    [(11.9, "late", "rstd", 0), (41.8, "late", "rstd", 1)],
)
SP_TABLE = in_order(
    [(0.0, "next", "xT", 0), (0.1, "attn", "pack", 1), (0.2, "next", "adj", 0), (3.0, "attn", "x", 0), (6.0, "next", "bounce", 0), (9.0, "next", "bounce", 1),
     (17.0, "attn", "M", 0), (17.5, "mid", "codesT", 0), (48.0, "attn", "M", 1),
     (42.0, "mid", "codes", 0), (51.0, "next", "pack", 0), (51.6, "next", "adjT", 0), (52.0, "late", "store", 0),
     (58.6, "next", "spill", 0)],
)


def build(nc, x, xT, adj, adjT, weights, vec_rows, vec_cols, out):
    with ExitStack() as ctx:
        def sb(name, shape, dt=F32):
            return ctx.enter_context(nc.sbuf_tensor(name, shape, dt))

        def sem(name):
            return ctx.enter_context(nc.semaphore(name))

        wts = sb("wts", [P, W_ALL])
        cols = sb("cols", [P, len(VECS)])
        rows = sb("rows", [P, len(ROWS), DIM])
        gat_ext = sb("gat_ext", [P, DIM + 1])
        gat_right = sb("gat_right", [P, P])
        a_right = sb("a_right", [P, P])
        ff_bias = sb("ff_bias", [P, DIM])
        not_self = sb("not_self", [P, P], BF16)
        ident16 = sb("ident16", [P, P], BF16)
        ones16 = sb("ones16", [P, 2], BF16)
        eps_tile = sb("eps_tile", [P, TILES])
        half_tile = sb("half_tile", [P, TILES])

        adj_in = sb("adj_in", [P, TILES, NODES], I32)
        codes = [sb(f"codes{i}", [P, TILES, NODES], BF16) for i in range(2)]
        codesT_late = sb("codesT_late", [P, TILES, NODES], BF16)
        barred = [sb(f"barred{i}", [P, TILES, NODES], BF16) for i in range(2)]
        x_nat = sb("x_nat", [P, TILES, DIM])
        x_turned = sb("x_turned", [P, NODES])
        q_hi = sb("q_hi", [P, NODES], F32R)
        q_lo = sb("q_lo", [P, NODES], F32R)
        k_hi = sb("k_hi", [P, NODES], F32R)
        k_lo = sb("k_lo", [P, NODES], F32R)
        q_pack = sb("q_pack", [SHIFT_ROW + 1, HEADS, NODES], F32R)
        k_pack = sb("k_pack", [SHIFT_ROW + 1, HEADS, NODES], F32R)
        values = [sb(f"values{i}", [P, TILES, HEADS, SLOT]) for i in range(2)]
        maxima = sb("maxima", [P, HEADS * TILES])
        shift = sb("shift", [GROUP * TILES, P], F32R)
        probs = [sb(f"probs{i}", [P, GROUP, NODES]) for i in range(4)]
        ctx_T = [sb(f"ctx_T{i}", [P, NODES]) for i in range(GROUPS)]

        ctx_sum = sb("ctx_sum", [P, TILES * HEADS])
        mid_T = [sb(f"mid_T{i}", [P, NODES]) for i in range(2)]
        late_T = [sb(f"late_T{i}", [P, NODES]) for i in range(2)]
        big_a = sb("big_a", [P, TILES, NODES])
        big_b = sb("big_b", [P, TILES, NODES])
        agg_T = [sb(f"agg_T{i}", [P, NODES]) for i in range(2)]
        x_bo_y1 = sb("x_bo_y1", [P, TILES, DIM])
        x1_y2 = sb("x1_y2", [P, TILES, DIM])
        x_b2 = sb("x_b2", [P, TILES, DIM])
        z_mid = sb("z_mid", [P, TILES, DIM])
        resid_mid = sb("resid_mid", [P, TILES, DIM])
        y2_rest = sb("y2_rest", [P, TILES, DIM])
        y3 = sb("y3", [P, TILES, DIM])
        pre = sb("pre", [P, TILES, DIM])
        act_out = sb("act_out", [P, TILES, DIM])
        resid_late = sb("resid_late", [P, TILES, DIM])
        stats = {r: sb(f"stats_{r}", [P, TILES, 6]) for r in ("mid", "late")}
        moments = {r: sb(f"moments_{r}", [P, TILES, 2]) for r in ("mid", "late")}
        spread = {r: sb(f"spread_{r}", [P, TILES]) for r in ("mid", "late")}
        rstd = {r: sb(f"rstd_{r}", [P, TILES]) for r in ("mid", "late")}
        no_edge = sb("no_edge", [P, TILES, NODES], BF16)
        is_one = sb("is_one", [P, TILES, NODES], BF16)
        is_rel = [sb(f"is_rel{i}", [P, TILES, NODES], F16) for i in range(2)]
        h_ext = sb("h_ext", [P, TILES, DIM + 1])
        gat_max = sb("gat_max", [P, TILES])
        gat_top = sb("gat_top", [P, TILES])
        gat_low = sb("gat_low", [P, TILES])
        gat_total = sb("gat_total", [P, TILES])
        gat_inv = sb("gat_inv", [P, TILES])
        degree = sb("degree", [P, TILES])
        deg_inv = sb("deg_inv", [P, TILES])
        part_hi = sb("part_hi", [P, TILES, DIM], F16)
        part_lo = sb("part_lo", [P, TILES, DIM], F16)
        h_parts = [is_rel[0][:, i, :].bitcast(BF16).rearrange("p (t c) -> p t c", t=TILES) for i in range(3)]

        RING = 3
        ring = [ctx.enter_context(nc.psum_tensor(f"ring{i}", [P, 512], F32)) for i in range(RING)]
        C_bank = ctx.enter_context(nc.psum_tensor("C_bank", [P, 512], F32))
        A_pair = ctx.enter_context(nc.psum_tensor("A_pair", [P, 2, 512], F32))
        A = [A_pair[:, 0, :], A_pair[:, 1, :]]
        B = [ctx.enter_context(nc.psum_tensor(f"B_bank{i}", [P, 512], F32))[:, :] for i in range(2)]

        bounce = [nc.dram_tensor(f"bounce{i}", [4, P, NODES], F32).ap() for i in range(2)]
        codes_dram = [nc.dram_tensor(f"codes_dram{i}", [GRAPHS, P, TILES * NODES], BF16).ap() for i in range(2)]

        def w(name, a=0, b=None):
            lo, hi = W_COLS[name]
            return wts[:, lo + a:(hi if b is None else lo + b)]

        def col(name):
            n = VECS.index(name)
            return cols[:, n:n + 1]

        def row4(name):
            return rows[:, ROWS.index(name):ROWS.index(name) + 1, :].broadcast_to((P, TILES, DIM))

        def nat(bank):
            return bank.rearrange("p (t c) -> p t c", t=TILES)

        weights_in = sem("weights_in")
        values_zeroed = sem("values_zeroed")
        dve_consts = sem("dve_consts")
        pool_consts = sem("pool_consts")
        ff_bias_ready = sem("ff_bias_ready")
        gat_a_ready = sem("gat_a_ready")
        gat_w_psum = sem("gat_w_psum")
        gat_w_ready = sem("gat_w_ready")
        gate = sem("gate")
        adj_loaded = sem("adj_loaded")
        x_loaded = sem("x_loaded")
        xT_loaded = sem("xT_loaded")
        coded = sem("coded")
        spilled = sem("spilled")
        allow = sem("allow")
        no_edge_ready = sem("no_edge_ready")
        q_proj, k_proj, v_proj = sem("q_proj"), sem("k_proj"), sem("v_proj")
        qk_hi = sem("qk_hi")
        qk_lo = sem("qk_lo")
        v_ready = sem("v_ready")
        bounced = sem("bounced")
        packed = [sem(f"packed{i}") for i in range(GROUPS)]
        scored = sem("scored")
        maxed = sem("maxed")
        max_turned = sem("max_turned")
        shift_ready = sem("shift_ready")
        shift_packed = sem("shift_packed")
        shifted = sem("shifted")
        exped = sem("exped")
        weighted = sem("weighted")
        ctx_copied = sem("ctx_copied")
        resid_ready = {r: sem(f"resid_ready_{r}") for r in ("mid", "late")}
        stats_ready = {r: sem(f"stats_ready_{r}") for r in ("mid", "late")}
        moments_ready = {r: sem(f"moments_ready_{r}") for r in ("mid", "late")}
        spread_ready = {r: sem(f"spread_ready_{r}") for r in ("mid", "late")}
        rstd_ready = {r: sem(f"rstd_ready_{r}") for r in ("mid", "late")}
        normed = {r: sem(f"normed_{r}") for r in ("mid", "late")}
        ctx_turned = sem("ctx_turned")
        ctx_inv = sem("ctx_inv")
        ctx_scaled = sem("ctx_scaled")
        ctx_back = sem("ctx_back")
        ctx_back_in = sem("ctx_back_in")
        x_bo_ready = sem("x_bo_ready")
        x_b2_ready = sem("x_b2_ready")
        wo_done = sem("wo_done")
        z_turned = sem("z_turned")
        z_in = sem("z_in")
        z_scaled = sem("z_scaled")
        x1_ready = sem("x1_ready")
        ff1_done = sem("ff1_done")
        ff1_in = sem("ff1_in")
        ff2_done = sem("ff2_done")
        z2_scaled = sem("z2_scaled")
        y1_turned = sem("y1_turned")
        y1_in = sem("y1_in")
        gat_right_done = sem("gat_right_done")
        h_done = sem("h_done")
        h_in = sem("h_in")
        gat_maxed = sem("gat_maxed")
        gat_sum_max = sem("gat_sum_max")
        gat_top_ready = sem("gat_top_ready")
        gat_low_ready = sem("gat_low_ready")
        gat_e = sem("gat_e")
        gat_leaky = sem("gat_leaky")
        gat_exped = sem("gat_exped")
        gat_pT = sem("gat_pT")
        gat_pT_in = sem("gat_pT_in")
        gat_done = sem("gat_done")
        gat_inv_ready = sem("gat_inv_ready")
        hi_ready = sem("hi_ready")
        lo_ready = sem("lo_ready")
        y2_bias = sem("y2_bias")
        codesT_back = sem("codesT_back")
        codes_back = sem("codes_back")
        rel_mask = sem("rel_mask")
        agg_done = sem("agg_done")
        agg_in = sem("agg_in")
        rel_done = sem("rel_done")
        one_mask = sem("one_mask")
        y3_hi = sem("y3_hi")
        y3_lo = sem("y3_lo")
        y3_turned = sem("y3_turned")
        y3_in = sem("y3_in")
        near_done = sem("near_done")
        near_in = sem("near_in")
        deg_done = sem("deg_done")
        deg_ready = sem("deg_ready")
        deg_inv_ready = sem("deg_inv_ready")
        root_done = sem("root_done")
        near_w_done = sem("near_w_done")
        root_in = sem("root_in")
        pre_ready = sem("pre_ready")
        pre_low = sem("pre_low")
        pre_exp = sem("pre_exp")
        elu_ready = sem("elu_ready")
        part_ready = sem("part_ready")
        rest1 = sem("rest1")
        part3 = sem("part3")
        h1_turned = sem("h1_turned")
        h1_in = sem("h1_in")
        stored = sem("stored")

        def first(g):
            return isinstance(g, int) and g == 0

        def alone(eng, s, value):
            eng.wait_ge(s, value)
            eng.sem_inc(gate, 1)

        USES = [(what, n) for _, _, what, n in in_order(SCORES, SHIFTED, MAXIMA)]
        USED_BY = {"S": (maxed, SCORE_TILES), "T": (exped, SCORE_TILES), "M": (shift_ready, GROUPS)}

        def bank_of(what, n):
            return ring[USES.index((what, n)) % RING]

        def wait_bank(eng, g, what, n):
            u = USES.index((what, n)) - RING
            if u < 0 and first(g):
                return
            before, m = USES[u % len(USES)]
            signal, per = USED_BY[before]
            eng.wait_ge(signal, g * per + (m + 1 - (per if u < 0 else 0)))

        def steps(eng, table, piece):
            def step(i, parity, roles):
                graph = {"next": (i + 1, 1 - parity), "attn": (i, parity), "mid": (i - 1, 1 - parity),
                         "late": (i - 2, parity)}
                for _, role, what, n in table:
                    if role in roles:
                        piece(role, *graph[role], what, n)

            step(0, 0, ("next", "attn"))
            step(1, 1, ("next", "attn", "mid"))
            step(2, 0, ("next", "attn", "mid", "late"))
            with eng.Fori(0, (GRAPHS - 4) // 2) as n:
                step(n * 2 + 3, 1, ("next", "attn", "mid", "late"))
                step(n * 2 + 4, 0, ("next", "attn", "mid", "late"))
            step(GRAPHS - 1, 1, ("attn", "mid", "late"))
            step(GRAPHS, 0, ("mid", "late"))
            step(GRAPHS + 1, 1, ("late",))

        block = ctx.enter_context(nc.Block())

        @block.sync
        def _(sp):
            sp.dma_start(wts[:, :], weights).then_inc(weights_in, 16)
            sp.dma_start(cols[:, :], vec_cols).then_inc(weights_in, 16)
            sp.dma_start(rows[:, :, :].rearrange("p a b -> p (a b)"),
                         vec_rows.partition_broadcast(P)).then_inc(weights_in, 16)

            def flat(t):
                return t.rearrange("p t n -> p (t n)")

            def piece(role, g, p, what, n):
                if what == "x":
                    if not first(g):
                        sp.wait_ge(x_bo_ready, g)
                        sp.wait_ge(x_b2_ready, g)
                    sp.dma_start(flat(x_nat[:, :, :]), x[g]).then_inc(x_loaded, 16)
                if what == "xT":
                    if not first(g):
                        sp.wait_ge(v_proj, g)
                    sp.dma_start(x_turned[:, :], xT[g]).then_inc(xT_loaded, 16)
                if what == "adj":
                    if not first(g):
                        sp.wait_ge(coded, g * 2)
                    sp.dma_start(flat(adj_in[:, :, :]), adj[g]).then_inc(adj_loaded, 16)
                if what == "adjT":
                    sp.wait_ge(coded, g * 2 + 1)
                    sp.dma_start(flat(adj_in[:, :, :]), adjT[g]).then_inc(adj_loaded, 16)
                    sp.dma_start(codes_dram[0][g], flat(codes[0][:, :, :])).then_inc(spilled, 16)
                if what == "spill":
                    sp.wait_ge(coded, g * 2 + 2)
                    sp.dma_start(codes_dram[1][g], flat(codes[1][:, :, :])).then_inc(spilled, 16)
                if what == "codesT":
                    alone(sp, spilled, g * 32 + 32)
                    if not first(g):
                        sp.wait_ge(rel_mask, g * 4)
                    sp.dma_start(flat(codesT_late[:, :, :]), codes_dram[1][g]).then_inc(codesT_back, 16)
                if what == "codes":
                    if not first(g):
                        sp.wait_ge(near_done, g * 2)
                        sp.wait_ge(deg_done, g)
                    sp.dma_start(flat(is_one[:, :, :]), codes_dram[0][g]).then_inc(codes_back, 16)
                if what == "bounce":
                    for s, src in ((qk_hi, (q_hi, k_hi)[n]), (qk_lo, (q_lo, k_lo)[n])):
                        sp.wait_ge(s, g * 2 + (n + 1))
                        sp.dma_start(bounce[p][2 * n + (s is qk_lo)], src[:, :].bitcast(F32)).then_inc(bounced, 16)
                if what == "pack":
                    alone(sp, bounced, g * 64 + 64)
                    if not first(g):
                        sp.wait_ge(shifted, g * 32 + (16 * (n + 1) - 32))
                    for dst, parts in ((q_pack, (0, 0, 1, 1)), (k_pack, (2, 3, 2, 3))):
                        for b, part in enumerate(parts):
                            src = bounce[p][part].rearrange("(h d) n -> d h n", h=HEADS)
                            sp.dma_start(dst[b * HEAD:(b + 1) * HEAD, n * GROUP:(n + 1) * GROUP, :].bitcast(F32),
                                         src[:, n * GROUP:(n + 1) * GROUP, :]).then_inc(packed[n], 16)
                if what == "M":
                    sp.wait_ge(shift_ready, g * 2 + (n + 1))
                    sp.dma_start(q_pack[SHIFT_ROW:SHIFT_ROW + 1, n * GROUP:(n + 1) * GROUP, :]
                                 .rearrange("o h (t q) -> o (h t) q", t=TILES).bitcast(F32),
                                 shift[:, :].bitcast(F32)).then_inc(shift_packed, 16)
                if what == "store":
                    sp.wait_ge(normed["late"], g * 2 + 2)
                    sp.dma_start(out[g], flat(resid_late[:, :, :])).then_inc(stored, 16)

            for what, n in (("xT", 0), ("adj", 0), ("bounce", 0), ("bounce", 1), ("adjT", 0), ("spill", 0)):
                piece("next", 0, 0, what, n)
            sp.wait_ge(dve_consts, 2)
            piece("next", 0, 0, "pack", 0)
            steps(sp, SP_TABLE, piece)
            sp.wait_ge(stored, 16 * GRAPHS)
            sp.wait_ge(spilled, 32 * GRAPHS)
            sp.wait_ge(bounced, 64 * GRAPHS)

        @block.tensor
        def _(pe):
            ident = w("ident")

            pe.wait_ge(weights_in, 48)
            pe.wait_ge(gat_a_ready, 1)
            nc.tensor.matmul(A[1][:, 0:P], w("gatT"), a_right[:, :], start=True, stop=True)
            nc.tensor.matmul(A[1][:, P:P + 1], w("gatT"), col("a_l"), start=True, stop=True).then_inc(gat_w_psum, 1)
            pe.wait_ge(gat_w_ready, 1)

            def turn(dst, src):
                for t in range(TILES):
                    last = nc.tensor.transpose(dst[:, t * P:(t + 1) * P], src[:, t, :], ident)
                return last

            def apply_w(dst, srcT, wt):
                for t in range(TILES):
                    last = nc.tensor.matmul(nat(dst)[:, t, :], srcT[:, t * P:(t + 1) * P], wt, start=True, stop=True)
                return last

            def project(g, n):
                if n == 0:
                    pe.wait_ge(xT_loaded, g * 16 + 16)
                    if not (isinstance(g, int) and g < 2):
                        pe.wait_ge(ctx_copied, g * 2 - 2)
                    nc.tensor.matmul(C_bank[:, :], w("q"), x_turned[:, :], start=True, stop=True).then_inc(q_proj, 1)
                if n == 1:
                    pe.wait_ge(qk_lo, g * 2 + 1)
                    nc.tensor.matmul(C_bank[:, :], w("k"), x_turned[:, :], start=True, stop=True).then_inc(k_proj, 1)
                if n == 2:
                    pe.wait_ge(qk_lo, g * 2 + 2)
                    apply_w(C_bank[:, :], x_turned, w("v")).then_inc(v_proj, 1)

            def attention(g, p, what, n):
                if what == "S":
                    h, t = divmod(n, TILES)
                    if n % (GROUP * TILES) == 0:
                        pe.wait_ge(packed[h // GROUP], g * 128 + 128)
                    wait_bank(pe, g, "S", n)
                    nc.tensor.matmul(bank_of("S", n)[:, :], q_pack[0:ONE_ROW + 1, h, t * P:(t + 1) * P],
                                     k_pack[0:ONE_ROW + 1, h, :], start=True, stop=True).then_inc(scored, 1)
                if what == "M":
                    pe.wait_ge(maxed, g * 32 + 16 * (n + 1))
                    wait_bank(pe, g, "M", n)
                    nc.tensor.transpose(bank_of("M", n)[0:GROUP * TILES, 0:P], maxima[:, n * 16:(n + 1) * 16],
                                        ident).then_inc(max_turned, 1)
                if what == "T":
                    slot, j = divmod(n, GROUP)
                    grp, kt = divmod(slot, TILES)
                    h = grp * GROUP + j
                    if kt == 0 and j == 0:
                        pe.wait_ge(shift_packed, g * 32 + 16 * (grp + 1))
                        if grp == 0:
                            pe.wait_ge(allow, g * 3 + 3)
                    wait_bank(pe, g, "T", n)
                    nc.tensor.matmul(bank_of("T", n)[:, :], k_pack[:, h, kt * P:(kt + 1) * P], q_pack[:, h, :],
                                     start=True, stop=False)
                    nc.tensor.matmul(bank_of("T", n)[:, :], ident16[:, :], barred[p][:, kt, :], start=False,
                                     stop=True).then_inc(shifted, 1)
                if what == "V":
                    grp, kt = divmod(n, TILES)
                    if n == 0:
                        if isinstance(g, int) and g == GRAPHS - 1:
                            pe.wait_ge(v_ready, GRAPHS)
                            pe.wait_ge(ctx_copied, 2 * g)
                        else:
                            pe.wait_ge(v_ready, g + 2)
                    if n == TILES:
                        pe.wait_ge(ctx_copied, g * 2 + 1)
                    pe.wait_ge(exped, g * SCORE_TILES + GROUP * (n + 1))
                    for j in range(GROUP):
                        last = nc.tensor.matmul(C_bank[j * SLOT:(j + 1) * SLOT, :],
                                                values[p][:, kt, grp * GROUP + j, :], probs[n % 4][:, j, :],
                                                start=(kt == 0), stop=(kt == TILES - 1),
                                                tile_position=(0, j * SLOT))
                    last.then_inc(weighted, 1)

            def mid(g, p, what, n):
                if what == "turn_ctx":
                    pe.wait_ge(ctx_copied, g * 2 + 2)
                    if not first(g):
                        pe.wait_ge(resid_ready["mid"], g * 4)
                    for t in range(TILES):
                        for grp in range(GROUPS):
                            c = (t % 2) * 256 + grp * P
                            last = nc.tensor.transpose(A_pair[:, t // 2, c:c + P], ctx_T[grp][:, t * P:(t + 1) * P], ident)
                    last.then_inc(ctx_turned, 1)
                if what == "turn_back":
                    pe.wait_ge(ctx_scaled, g + 1)
                    turn(A[0], z_mid).then_inc(ctx_back, 1)
                if what == "wo":
                    pe.wait_ge(ctx_back_in, g + 1)
                    apply_w(A[1], mid_T[0], w("o")).then_inc(wo_done, 1)
                if what == "turn_z":
                    pe.wait_ge(normed["mid"], g * 4 + 1)
                    turn(A[0], z_mid).then_inc(z_turned, 1)
                if what == "ff1":
                    if n == 0:
                        pe.wait_ge(z_in, g + 1)
                    if n >= 2:
                        pe.wait_ge(ff1_in, g * 4 + (n - 1))
                    nc.tensor.matmul(A[(n + 1) % 2], w("ff1", n * P, (n + 1) * P), mid_T[1][:, :],
                                     start=True, stop=True).then_inc(ff1_done, 1)
                if what == "ff2":
                    if n == 0:
                        pe.wait_ge(ff1_in, g * 4 + 4)
                    for f in range(FT):
                        last = nc.tensor.matmul(nat(A[1])[:, n, :], big_a[:, f, n * P:(n + 1) * P],
                                                w("ff2", f * P, (f + 1) * P), start=(f == 0), stop=(f == FT - 1))
                    if n == TILES - 1:
                        last.then_inc(ff2_done, 1)
                if what == "turn_y1":
                    pe.wait_ge(normed["mid"], g * 4 + 3)
                    turn(A[0], x_bo_y1).then_inc(y1_turned, 1)
                if what == "gat_right":
                    pe.wait_ge(y1_in, g + 1)
                    nc.tensor.matmul(A[1], gat_right[:, :], mid_T[0][:, :], start=True,
                                     stop=True).then_inc(gat_right_done, 1)
                if what == "gat_h":
                    if n == 1:
                        pe.wait_ge(h_in, g * 2 + 1)
                    for t in (2 * n, 2 * n + 1):
                        c = (t % 2) * 256
                        last = nc.tensor.matmul(A[0][:, c:c + DIM + 1], mid_T[0][:, t * P:(t + 1) * P],
                                                gat_ext[:, :], start=True, stop=True)
                    last.then_inc(h_done, 1)
                if what == "gat_turn":
                    if n == 0:
                        pe.wait_ge(gat_exped, g * 4 + 4)
                    if n >= 2:
                        pe.wait_ge(gat_pT_in, g * 4 + (n - 1))
                    for it in range(TILES):
                        last = nc.tensor.transpose(A[n % 2][:, it * P:(it + 1) * P],
                                                   big_b[:, it, n * P:(n + 1) * P], ident)
                    last.then_inc(gat_pT, 1)
                if what == "gat_sum":
                    if n == 0:
                        pe.wait_ge(gat_pT_in, g * 4 + 4)
                    for jt in range(TILES):
                        last = nc.tensor.matmul(nat(A[0])[:, n, :], big_a[:, jt, n * P:(n + 1) * P],
                                                h_ext[:, jt, 0:DIM], start=(jt == 0), stop=(jt == TILES - 1))
                    if n == TILES - 1:
                        last.then_inc(gat_done, 1)

            def late(g, p, what, n):
                if what == "agg":
                    r, half = divmod(n, 2)
                    if half == 0:
                        if r == 0:
                            pe.wait_ge(lo_ready, g + 1)
                            if not first(g):
                                pe.wait_ge(pre_ready, g * 2)
                        else:
                            pe.wait_ge(agg_in, g * 4 + r)
                        pe.wait_ge(rel_mask, g * 4 + (r + 1))
                    for mt in (2 * half, 2 * half + 1):
                        for k, part in enumerate((part_hi, part_lo)):
                            last = nc.tensor.matmul(B[0], part[:, mt, :], is_rel[r % 2][:, mt, :],
                                                    start=(mt == 0 and k == 0), stop=(mt == TILES - 1 and k == 1))
                    if half == 1:
                        last.then_inc(agg_done, 1)
                if what == "rel":
                    pe.wait_ge(agg_in, g * 4 + (n + 1))
                    for t in range(TILES):
                        last = nc.tensor.matmul(nat(B[1])[:, t, :], agg_T[n % 2][:, t * P:(t + 1) * P],
                                                w("rel", n * P, (n + 1) * P), start=(n == 0 and t == 0),
                                                stop=(n == RELS - 1), skip_group_check=True)
                    last.then_inc(rel_done, 1)
                if what == "turn_y3":
                    pe.wait_ge(normed["late"], g * 2 + 1)
                    turn(B[0], y3).then_inc(y3_turned, 1)
                if what == "near1":
                    if n == 0:
                        pe.wait_ge(y3_lo, g + 1)
                        pe.wait_ge(one_mask, g + 1)
                    for it in (2 * n, 2 * n + 1):
                        for k, part in enumerate((part_hi, part_lo)):
                            last = nc.tensor.matmul(B[1], part[:, it, :], is_one[:, it, :],
                                                    start=(it == 0 and k == 0), stop=(it == TILES - 1 and k == 1))
                    if n == 1:
                        last.then_inc(near_done, 1)
                if what == "degree":
                    pe.wait_ge(y3_in, g + 1)
                    for jt in range(TILES):
                        for it in range(TILES):
                            last = nc.tensor.matmul(B[0][:, 2 * jt:2 * jt + 2], is_one[:, it, jt * P:(jt + 1) * P],
                                                    ones16[:, :], start=(it == 0), stop=(it == TILES - 1))
                    last.then_inc(deg_done, 1)
                if what == "root":
                    pe.wait_ge(near_in if n == 0 else h1_in, g * (2 - n) + 1)
                    apply_w(B[1], late_T[0], w(("root1", "root2")[n])).then_inc(root_done, 1)
                if what == "near_w":
                    if n == 0:
                        pe.wait_ge(deg_ready, g + 1)
                    else:
                        pe.wait_ge(near_in, g * 2 + 2)
                    apply_w(B[0], late_T[1], w(("near1", "near2")[n])).then_inc(near_w_done, 1)
                if what == "turn_h1":
                    pe.wait_ge(elu_ready, g * 2 + 1)
                    turn(B[1], act_out).then_inc(h1_turned, 1)
                if what == "near2":
                    if n == 0:
                        pe.wait_ge(part_ready, g * 2 + 1)
                    if n == 1:
                        pe.wait_ge(part_ready, g * 2 + 2)
                    if n == 2:
                        pe.wait_ge(part3, g + 1)
                    for it in range(TILES):
                        last = nc.tensor.matmul(B[0], h_parts[n][:, it, :], is_one[:, it, :],
                                                start=(it == 0 and n == 0), stop=(it == TILES - 1 and n == 2))
                    if n == 2:
                        last.then_inc(near_done, 1)

            def piece(role, g, p, what, n):
                if role == "next":
                    project(g, n)
                elif role == "attn" or what == "V":
                    attention(g, p, what, n)
                elif role == "mid":
                    mid(g, p, what, n)
                else:
                    late(g, p, what, n)

            for n in range(3):
                project(0, n)
            pe.wait_ge(dve_consts, 2)
            steps(pe, PE_TABLE, piece)

        @block.scalar
        def _(act):
            act.wait_ge(weights_in, 48)
            act.wait_ge(gat_w_psum, 1)
            nc.scalar.activation(gat_right[:, :], A[1][:, 0:P], ACT.Copy)
            nc.scalar.activation(gat_ext[:, 0:DIM], w("gat"), ACT.Copy)
            nc.scalar.activation(gat_ext[:, DIM:DIM + 1], A[1][:, P:P + 1], ACT.Copy).then_inc(gat_w_ready, 1)

            def piece(role, g, p, what, n):
                if what == "proj":
                    if n == 0 and not first(g):
                        act.wait_ge(bounced, g * 64)
                    act.wait_ge((q_proj, k_proj)[n], g + 1)
                    nc.scalar.activation((q_hi, k_hi)[n][:, :], C_bank[:, :], ACT.Identity,
                                         bias=col(("bq", "bk")[n])).then_inc(qk_hi, 1)
                if what == "M":
                    act.wait_ge(max_turned, g * 2 + (n + 1))
                    if not (first(g) and n == 0):
                        act.wait_ge(shift_packed, g * 32 + 16 * n)
                    nc.scalar.activation(shift[:, :], bank_of("M", n)[0:GROUP * TILES, 0:P], ACT.Copy,
                                         scale=-1.0).then_inc(shift_ready, 1)
                if what == "T":
                    slot, j = divmod(n, GROUP)
                    if j == 0 and not (first(g) and slot < 4):
                        act.wait_ge(weighted, g * 8 + (slot - 3))
                    act.wait_ge(shifted, g * 32 + (n + 1))
                    nc.scalar.activation(probs[slot % 4][:, j, :], bank_of("T", n)[:, :], ACT.Exp,
                                         scale=SCALE).then_inc(exped, 1)
                if what == "C":
                    act.wait_ge(weighted, g * 8 + 4 * (n + 1))
                    if not first(g):
                        act.wait_ge(ctx_turned, g)
                    nc.scalar.activation(ctx_T[n][:, :], C_bank[:, :], ACT.Copy).then_inc(ctx_copied, 1)
                if what == "back":
                    act.wait_ge(ctx_back, g + 1)
                    nc.scalar.activation(mid_T[0][:, :], A[0], ACT.Copy).then_inc(ctx_back_in, 1)
                if what == "z":
                    act.wait_ge(z_turned, g + 1)
                    nc.scalar.activation(mid_T[1][:, :], A[0], ACT.Identity, bias=col("b1"),
                                         scale=col("g1")).then_inc(z_in, 1)
                if what == "ff1":
                    act.wait_ge(ff1_done, g * 4 + (n + 1))
                    nc.scalar.activation(big_a[:, n, :], A[(n + 1) % 2], ACT.Relu, bias=col(f"ff1_{n}")).then_inc(ff1_in, 1)
                if what == "y1":
                    act.wait_ge(y1_turned, g + 1)
                    nc.scalar.activation(mid_T[0][:, :], A[0], ACT.Copy).then_inc(y1_in, 1)
                if what == "h":
                    act.wait_ge(h_done, g * 2 + (n + 1))
                    nc.scalar.activation(h_ext[:, 2 * n:2 * n + 2, :],
                                         A[0].rearrange("p (t c) -> p t c", t=2)[:, :, 0:DIM + 1],
                                         ACT.Copy).then_inc(h_in, 1)
                if what == "gat_exp":
                    if n == 0:
                        act.wait_ge(gat_leaky, g + 1)
                        act.wait_ge(gat_low_ready, g + 1)
                    nc.scalar.activation(big_b[:, n, :], big_b[:, n, :], ACT.Exp, bias=gat_low[:, n:n + 1],
                                         accum_out=gat_total[:, n:n + 1]).then_inc(gat_exped, 1)
                if what == "gat_turn":
                    act.wait_ge(gat_pT, g * 4 + (n + 1))
                    nc.scalar.activation(big_a[:, n, :], A[n % 2], ACT.Copy).then_inc(gat_pT_in, 1)
                if what == "high":
                    if role == "mid":
                        act.wait_ge(normed["mid"], g * 4 + 4)
                        if not first(g):
                            act.wait_ge(near_done, g * 2 - 1)
                        nc.scalar.activation(part_hi[:, :, :], x1_y2[:, :, :], ACT.Copy, scale=UP).then_inc(hi_ready, 1)
                    else:
                        act.wait_ge(normed["late"], g * 2 + 1)
                        nc.scalar.activation(part_hi[:, :, :], y3[:, :, :], ACT.Copy, scale=UP).then_inc(y3_hi, 1)
                if what == "agg":
                    act.wait_ge(agg_done, g * 4 + (n + 1))
                    if n >= 2:
                        act.wait_ge(rel_done, g * 4 + (n - 1))
                    nc.scalar.activation(agg_T[n % 2][:, :], B[0], ACT.Copy, scale=1.0 / UP).then_inc(agg_in, 1)
                if what == "y3":
                    act.wait_ge(y3_turned, g + 1)
                    nc.scalar.activation(late_T[0][:, :], B[0], ACT.Copy).then_inc(y3_in, 1)
                if what == "near":
                    act.wait_ge(near_done, g * 2 + (n + 1))
                    nc.scalar.activation(late_T[1][:, :], B[1 - n], ACT.Copy, scale=(1.0 / UP, 1.0)[n]).then_inc(near_in, 1)
                if what == "elu":
                    act.wait_ge(pre_low, g * 2 + (n + 1))
                    nc.scalar.activation(act_out[:, :, :], act_out[:, :, :], ACT.Exp).then_inc(pre_exp, 1)
                if what == "part":
                    if n == 0:
                        act.wait_ge(elu_ready, g * 2 + 1)
                        nc.scalar.activation(h_parts[0], act_out[:, :, :], ACT.Copy).then_inc(part_ready, 1)
                    else:
                        act.wait_ge(rest1, g + 1)
                        nc.scalar.activation(h_parts[1], y2_rest[:, :, :], ACT.Copy).then_inc(part_ready, 1)
                if what == "h1":
                    act.wait_ge(h1_turned, g + 1)
                    nc.scalar.activation(late_T[0][:, :], B[1], ACT.Copy).then_inc(h1_in, 1)

            for n in range(2):
                piece("next", 0, 0, "proj", n)
            steps(act, ACT_TABLE, piece)

        @block.vector
        def _(dve):
            for p in range(2):
                nc.vector.memset(values[p][:, :, :, :], 0.0).then_inc(values_zeroed, 1)
            dve.wait_ge(values_zeroed, 2)
            for p in range(2):
                nc.vector.memset(values[p][:, :, :, HEAD:HEAD + 1], 1.0)
            nc.vector.memset(q_pack[PACK:SHIFT_ROW + 1, :, :].bitcast(F32), 0.0)
            nc.vector.memset(k_pack[PACK:SHIFT_ROW + 1, :, :].bitcast(F32), 1.0)
            nc.vector.memset(ones16[:, :], 1.0).then_inc(dve_consts, 1)
            dve.wait_ge(weights_in, 48)
            nc.vector.tensor_copy(a_right[:, :], col("a_r").broadcast_to((P, P))).then_inc(gat_a_ready, 1)
            nc.vector.tensor_copy(ident16[:, :], w("ident"))
            nc.vector.tensor_scalar(not_self[:, :], w("ident"), -1.0, 1.0, ALU.mult, ALU.add).then_inc(dve_consts, 1)
            dve.wait_ge(dve_consts, 2)

            def next_graph(g, p, what, n):
                if what == "codes":
                    dve.wait_ge(adj_loaded, g * 32 + 16 * (n + 1))
                    if not first(g):
                        dve.wait_ge(spilled, g * 32 + (16 * (n + 1) - 32))
                        dve.wait_ge(allow, g * 3)
                        dve.wait_ge(no_edge_ready, g)
                    nc.vector.tensor_scalar(codes[n][:, :, :], adj_in[:, :, :], 0.0, RELS + 1.0, ALU.max,
                                            ALU.min).then_inc(coded, 1)
                if what == "no_edge":
                    dve.wait_ge(coded, g * 2 + 1)
                    if not first(g):
                        dve.wait_ge(gat_maxed, g * 4)
                    nc.vector.tensor_scalar(no_edge[:, :, :], codes[0][:, :, :], 0.5, NEG_BIG / ALPHA, ALU.is_lt,
                                            ALU.mult).then_inc(no_edge_ready, 1)
                if what == "barred" and n == 0:
                    dve.wait_ge(coded, g * 2 + 2)
                    if not (isinstance(g, int) and g < 2):
                        dve.wait_ge(shifted, g * 32 - 32)
                    nc.vector.tensor_tensor(barred[p][:, :, :], codes[0][:, :, :], codes[1][:, :, :],
                                            ALU.max).then_inc(allow, 1)
                if what == "barred" and n == 1:
                    dve.wait_ge(allow, g * 3 + 1)
                    nc.vector.tensor_scalar(barred[p][:, :, :], barred[p][:, :, :], 0.5, NEVER, ALU.is_lt,
                                            ALU.mult).then_inc(allow, 1)
                if what == "barred" and n == 2:
                    dve.wait_ge(allow, g * 3 + 2)
                    for t in range(TILES):
                        d = barred[p][:, t, t * P:(t + 1) * P]
                        last = nc.vector.tensor_tensor(d, d, not_self[:, :], ALU.mult)
                    last.then_inc(allow, 1)
                if what == "proj" and n < 2:
                    dve.wait_ge(qk_hi, g * 2 + (n + 1))
                    if n == 0 and not first(g):
                        dve.wait_ge(bounced, g * 64)
                    nc.vector.scalar_tensor_tensor((q_lo, k_lo)[n][:, :], C_bank[:, :], col(("bq", "bk")[n]),
                                                   (q_hi, k_hi)[n][:, :].bitcast(F32), ALU.add,
                                                   ALU.subtract).then_inc(qk_lo, 1)
                if what == "proj" and n == 2:
                    dve.wait_ge(v_proj, g + 1)
                    nc.vector.tensor_tensor(
                        values[p][:, :, :, 0:HEAD], C_bank[:, :].rearrange("p (t h d) -> p t h d", t=TILES, h=HEADS),
                        rows[:, 0:1, :].rearrange("p o (h d) -> p o h d", h=HEADS)
                        .broadcast_to((P, TILES, HEADS, HEAD)), ALU.add).then_inc(v_ready, 1)

            def attention(g, p, what, n):
                if what == "S":
                    if n == 0:
                        dve.wait_ge(allow, g * 3 + 3)
                    alone(dve, scored, g * 32 + (n + 1))
                    bank = bank_of("S", n)[:, :]
                    nc.vector.tensor_tensor_reduce(
                        out=bank, in0=bank, in1=barred[p][:, n % TILES, :], scale=1.0, scalar=-3e38, op0=ALU.add,
                        op1=ALU.max, accum_out=maxima[:, n:n + 1]).then_inc(maxed, 1)

            SOURCE = {"mid": resid_mid, "late": resid_late}
            RESULT = {"mid": (z_mid, z_mid, x_bo_y1, x1_y2), "late": (y3, resid_late)}

            def normalise(role, g, what, k):
                per, src, dst = len(RESULT[role]), SOURCE[role], RESULT[role][k]
                if what == "stats":
                    dve.wait_ge(resid_ready[role], g * per + (k + 1))
                    for t in range(TILES):
                        last = nc.vector.bn_stats(stats[role][:, t, :], src[:, t, :])
                    last.then_inc(stats_ready[role], 1)
                if what == "moments":
                    alone(dve, stats_ready[role], g * per + (k + 1))
                    for t in range(TILES):
                        last = nc.vector.bn_aggr(moments[role][:, t, :], stats[role][:, t, :])
                    last.then_inc(moments_ready[role], 1)
                if what == "apply":
                    dve.wait_ge(rstd_ready[role], g * per + (k + 1))
                    for t in range(TILES):
                        last = nc.vector.tensor_scalar(dst[:, t, :], src[:, t, :], moments[role][:, t, 0:1],
                                                       rstd[role][:, t:t + 1], ALU.subtract, ALU.mult)
                    last.then_inc(normed[role], 1)

            def mid(g, p, what, n):
                if what == "ctx":
                    dve.wait_ge(ctx_turned, g + 1)
                    src = A_pair[:, :, :].rearrange("p b (s d) -> p (b s) d", d=SLOT)
                    nc.vector.reciprocal(ctx_sum[:, :].rearrange("p (s o) -> p s o", o=1),
                                         src[:, :, HEAD:HEAD + 1]).then_inc(ctx_inv, 1)
                    dve.wait_ge(ctx_inv, g + 1)
                    nc.vector.tensor_tensor(
                        z_mid[:, :, :].rearrange("p t (h d) -> p (t h) d", h=HEADS), src[:, :, 0:HEAD],
                        ctx_sum[:, :].rearrange("p (s o) -> p s o", o=1).broadcast_to((P, TILES * HEADS, HEAD)),
                        ALU.mult).then_inc(ctx_scaled, 1)
                if what == "resid" and n == 0:
                    dve.wait_ge(wo_done, g + 1)
                    dve.wait_ge(x_bo_ready, g + 1)
                    nc.vector.tensor_tensor(resid_mid[:, :, :], nat(A[1]), x_bo_y1[:, :, :],
                                            ALU.add).then_inc(resid_ready["mid"], 1)
                if what == "resid" and n == 1:
                    dve.wait_ge(ff2_done, g + 1)
                    dve.wait_ge(x1_ready, g + 1)
                    nc.vector.tensor_tensor(resid_mid[:, :, :], nat(A[1]), x1_y2[:, :, :],
                                            ALU.add).then_inc(resid_ready["mid"], 1)
                if what == "gat_max":
                    if n == 0:
                        dve.wait_ge(gat_right_done, g + 1)
                        alone(dve, no_edge_ready, g + 1)
                    nc.vector.tensor_tensor_reduce(
                        out=big_b[:, n, :], in0=A[1], in1=no_edge[:, n, :], scale=1.0, scalar=-3e38,
                        op0=ALU.add, op1=ALU.max, accum_out=gat_max[:, n:n + 1]).then_inc(gat_maxed, 1)
                if what == "gat_top":
                    dve.wait_ge(gat_maxed, g * 4 + 4)
                    dve.wait_ge(h_in, g * 2 + 2)
                    m = gat_max[:, :].rearrange("p (t o) -> p t o", o=1)
                    nc.vector.tensor_tensor(m, m, h_ext[:, :, DIM:DIM + 1], ALU.add).then_inc(gat_sum_max, 1)
                if what == "gat_e":
                    last = nc.vector.tensor_scalar(big_b[:, n, :], big_b[:, n, :], h_ext[:, n, DIM:DIM + 1], None,
                                                   ALU.add)
                    if n == 0:
                        dve.wait_ge(gat_sum_max, g + 1)
                        nc.vector.scalar_tensor_tensor(gat_top[:, :], gat_max[:, :], ALPHA, gat_max[:, :], ALU.mult,
                                                       ALU.max).then_inc(gat_top_ready, 1)
                    if n == TILES - 1:
                        last.then_inc(gat_e, 1)
                if what == "leaky":
                    dve.wait_ge(gat_e, g + 1)
                    nc.vector.scalar_tensor_tensor(big_b[:, :, :], big_b[:, :, :], ALPHA, big_b[:, :, :], ALU.mult,
                                                   ALU.max).then_inc(gat_leaky, 1)
                    dve.wait_ge(gat_top_ready, g + 1)
                    nc.vector.tensor_scalar(gat_low[:, :], gat_top[:, :], -1.0, None,
                                            ALU.mult).then_inc(gat_low_ready, 1)
                if what == "gat_inv":
                    dve.wait_ge(gat_exped, g * 4 + 4)
                    nc.vector.reciprocal(gat_inv[:, :], gat_total[:, :]).then_inc(gat_inv_ready, 1)
                if what == "resid" and n == 3:
                    dve.wait_ge(gat_inv_ready, g + 1)
                    dve.wait_ge(gat_done, g + 1)
                    for t in range(TILES):
                        last = nc.vector.scalar_tensor_tensor(resid_mid[:, t, :], nat(A[0])[:, t, :],
                                                              gat_inv[:, t:t + 1], x_bo_y1[:, t, :], ALU.mult, ALU.add)
                    last.then_inc(resid_ready["mid"], 1)
                if what == "low":
                    dve.wait_ge(hi_ready, g + 1)
                    nc.vector.scalar_tensor_tensor(part_lo[:, :, :], x1_y2[:, :, :], UP, part_hi[:, :, :], ALU.mult,
                                                   ALU.subtract).then_inc(lo_ready, 1)

            def late(g, p, what, n):
                if what == "rel_mask":
                    if n == 0:
                        dve.wait_ge(codesT_back, g * 16 + 16)
                        if not first(g):
                            dve.wait_ge(near_done, g * 2)
                    if not (first(g) and n < 2):
                        dve.wait_ge(agg_done, g * 4 + (n - 1))
                    nc.vector.tensor_scalar(is_rel[n % 2][:, :, :], codesT_late[:, :, :], n + 1.0, None,
                                            ALU.is_equal).then_inc(rel_mask, 1)
                if what == "is_one":
                    dve.wait_ge(codes_back, g * 16 + 16)
                    nc.vector.tensor_scalar(is_one[:, :, :], is_one[:, :, :], 1.0, None,
                                            ALU.is_equal).then_inc(one_mask, 1)
                if what == "resid" and n == 0:
                    dve.wait_ge(rel_done, g * 4 + 4)
                    dve.wait_ge(y2_bias, g + 1)
                    if not first(g):
                        dve.wait_ge(stored, g * 16)
                    nc.vector.tensor_tensor(resid_late[:, :, :], nat(B[1]), y2_rest[:, :, :],
                                            ALU.add).then_inc(resid_ready["late"], 1)
                if what == "low":
                    dve.wait_ge(y3_hi, g + 1)
                    nc.vector.scalar_tensor_tensor(part_lo[:, :, :], y3[:, :, :], UP, part_hi[:, :, :], ALU.mult,
                                                   ALU.subtract).then_inc(y3_lo, 1)
                if what == "degree":
                    dve.wait_ge(deg_done, g + 1)
                    nc.vector.tensor_scalar(degree[:, :].rearrange("p (t o) -> p t o", o=1),
                                            B[0][:, 0:2 * TILES].rearrange("p (t o) -> p t o", o=2)[:, :, 0:1],
                                            1.0, None, ALU.max).then_inc(deg_ready, 1)
                    dve.wait_ge(deg_ready, g + 1)
                    nc.vector.reciprocal(deg_inv[:, :], degree[:, :]).then_inc(deg_inv_ready, 1)
                if what == "root":
                    dve.wait_ge(root_done, g * 2 + (n + 1))
                    nc.vector.tensor_tensor(pre[:, :, :], nat(B[1]), row4(("c1", "c2")[n]),
                                            ALU.add).then_inc(root_in, 1)
                if what == "pre":
                    dve.wait_ge(near_w_done, g * 2 + (n + 1))
                    dve.wait_ge(root_in, g * 2 + (n + 1))
                    dve.wait_ge(deg_inv_ready, g + 1)
                    for t in range(TILES):
                        last = nc.vector.scalar_tensor_tensor(pre[:, t, :], nat(B[0])[:, t, :], deg_inv[:, t:t + 1],
                                                              pre[:, t, :], ALU.mult, ALU.add)
                    last.then_inc(pre_ready, 1)
                if what == "elu_low":
                    dve.wait_ge(pre_ready, g * 2 + (n + 1))
                    nc.vector.tensor_scalar(act_out[:, :, :], pre[:, :, :], 0.0, None, ALU.min).then_inc(pre_low, 1)
                if what == "elu":
                    dve.wait_ge(pre_exp, g * 2 + (n + 1))
                    nc.vector.scalar_tensor_tensor(act_out[:, :, :], act_out[:, :, :], -1.0, pre[:, :, :], ALU.add,
                                                   ALU.max).then_inc(elu_ready, 1)
                if what == "part" and n == 0:
                    dve.wait_ge(part_ready, g * 2 + 1)
                    nc.vector.tensor_tensor(y2_rest[:, :, :], act_out[:, :, :], h_parts[0],
                                            ALU.subtract).then_inc(rest1, 1)
                if what == "part" and n == 1:
                    dve.wait_ge(part_ready, g * 2 + 2)
                    nc.vector.tensor_tensor(h_parts[2], y2_rest[:, :, :], h_parts[1],
                                            ALU.subtract).then_inc(part3, 1)
                if what == "resid" and n == 1:
                    dve.wait_ge(elu_ready, g * 2 + 2)
                    nc.vector.tensor_tensor(resid_late[:, :, :], act_out[:, :, :], y3[:, :, :],
                                            ALU.add).then_inc(resid_ready["late"], 1)

            def piece(role, g, p, what, n):
                if role == "next" or what == "no_edge":
                    next_graph(g, p, what, n)
                elif role == "attn":
                    if what != "M":
                        attention(g, p, what, n)
                elif what in NORM:
                    normalise(role, g, what, n)
                elif role == "mid":
                    mid(g, p, what, n)
                else:
                    late(g, p, what, n)

            for what, n in (("proj", 0), ("proj", 1), ("proj", 2), ("codes", 0), ("codes", 1),
                            ("barred", 0), ("barred", 1), ("barred", 2)):
                piece("next", 0, 0, what, n)
            steps(dve, DVE_TABLE, piece)

        @block.gpsimd
        def _(pool):
            nc.gpsimd.memset(eps_tile[:, :], EPS).then_inc(pool_consts, 1)
            nc.gpsimd.memset(half_tile[:, :], -0.5).then_inc(pool_consts, 1)
            pool.wait_ge(weights_in, 48)
            pool.wait_ge(pool_consts, 2)
            nc.gpsimd.tensor_tensor(ff_bias[:, :], rows[:, ROWS.index("b1"), :], rows[:, ROWS.index("ff2"), :],
                                    ALU.add).then_inc(ff_bias_ready, 1)
            pool.wait_ge(ff_bias_ready, 1)

            def piece(role, g, p, what, n):
                if what == "rstd":
                    per = 4 if role == "mid" else 2
                    pool.wait_ge(moments_ready[role], g * per + (n + 1))
                    nc.gpsimd.tensor_tensor(spread[role][:, :].rearrange("p (t o) -> p t o", o=1),
                                            moments[role][:, :, 1:2],
                                            eps_tile[:, :].rearrange("p (t o) -> p t o", o=1),
                                            ALU.add).then_inc(spread_ready[role], 1)
                    pool.wait_ge(spread_ready[role], g * per + (n + 1))
                    nc.gpsimd.tensor_tensor(rstd[role][:, :], spread[role][:, :], half_tile[:, :],
                                            ALU.pow).then_inc(rstd_ready[role], 1)
                if what == "x":
                    pool.wait_ge(x_loaded, g * 16 + 16)
                    if not first(g):
                        pool.wait_ge(resid_ready["mid"], g * 4)
                    nc.gpsimd.tensor_tensor(x_bo_y1[:, :, :], x_nat[:, :, :], row4("bo"), ALU.add).then_inc(x_bo_ready, 1)
                    nc.gpsimd.tensor_tensor(x_b2[:, :, :], x_nat[:, :, :], row4("b2"), ALU.add).then_inc(x_b2_ready, 1)
                if what == "x1":
                    pool.wait_ge(normed["mid"], g * 4 + 1)
                    if not first(g):
                        pool.wait_ge(lo_ready, g)
                    nc.gpsimd.tensor_tensor(x1_y2[:, :, :], z_mid[:, :, :], row4("g1"), ALU.mult).then_inc(z_scaled, 1)
                    pool.wait_ge(z_scaled, g + 1)
                    nc.gpsimd.tensor_tensor(x1_y2[:, :, :], x1_y2[:, :, :],
                                            ff_bias[:, :].rearrange("p (o c) -> p o c", o=1)
                                            .broadcast_to((P, TILES, DIM)), ALU.add).then_inc(x1_ready, 1)
                if what == "y1":
                    pool.wait_ge(normed["mid"], g * 4 + 2)
                    nc.gpsimd.tensor_tensor(z_mid[:, :, :], z_mid[:, :, :], row4("g2"), ALU.mult).then_inc(z2_scaled, 1)
                    pool.wait_ge(z2_scaled, g + 1)
                    nc.gpsimd.tensor_tensor(resid_mid[:, :, :], z_mid[:, :, :], x_b2[:, :, :],
                                            ALU.add).then_inc(resid_ready["mid"], 1)
                if what == "y2":
                    pool.wait_ge(normed["mid"], g * 4 + 4)
                    if not first(g):
                        pool.wait_ge(part3, g)
                    nc.gpsimd.tensor_tensor(y2_rest[:, :, :], x1_y2[:, :, :], row4("bias"), ALU.add).then_inc(y2_bias, 1)

            steps(pool, POOL_TABLE, piece)


_INPUTS = ("x", "xT", "adj", "adjT", "weights", "vec_rows", "vec_cols")


def kernel(**inputs):
    import numpy as np
    import concourse.bacc as bacc
    from concourse.bass_utils import run_bass_kernel_spmd

    a = {k: np.asarray(v) for k, v in inputs.items()}
    lay = np.ascontiguousarray
    f32 = np.float32

    def tiled(m):
        return lay(m.reshape(GRAPHS, TILES, P, m.shape[2]).transpose(0, 2, 1, 3)).reshape(GRAPHS, P, -1)

    wqkv = a["L0_gnn_Wqkv"]
    pieces = {
        "q": wqkv[0:DIM].T, "k": wqkv[DIM:2 * DIM].T, "v": wqkv[2 * DIM:].T, "o": a["L0_gnn_Wo"].T,
        "ff1": a["L0_gnn_W1"].T,
        "ff2": a["L0_gnn_W2"].T.reshape(FT, P, DIM).transpose(1, 0, 2).reshape(P, FT * DIM),
        "gat": a["L1_gnn_W"], "gatT": a["L1_gnn_W"].T,
        "rel": a["L2_gnn_weight"].transpose(1, 0, 2).reshape(P, RELS * DIM),
        "root1": a["L3_gnn_w_root1"], "near1": a["L3_gnn_w_rel1"][1],
        "root2": a["L3_gnn_w_root2"], "near2": a["L3_gnn_w_rel2"][1],
        "ident": np.eye(P, dtype=f32),
    }
    bqkv = a["L0_gnn_bqkv"]
    vec = {
        "bq": bqkv[0:DIM], "bk": bqkv[DIM:2 * DIM], "bv": bqkv[2 * DIM:], "bo": a["L0_gnn_bo"],
        "g1": a["L0_gnn_ln1_g"], "b1": a["L0_gnn_ln1_b"], "g2": a["L0_gnn_ln2_g"], "b2": a["L0_gnn_ln2_b"],
        "ff2": a["L0_gnn_b2"], "bias": a["L2_gnn_bias"], "c1": a["L3_gnn_b1"], "c2": a["L3_gnn_b2"],
        "a_l": a["L1_gnn_a"][0:DIM, 0], "a_r": a["L1_gnn_a"][DIM:, 0],
    }
    for f in range(FT):
        vec[f"ff1_{f}"] = a["L0_gnn_b1"][f * P:(f + 1) * P]
    arrays = {
        "x": tiled(a["x"]), "xT": lay(a["x"].transpose(0, 2, 1)),
        "adj": tiled(a["adj"]), "adjT": tiled(a["adj"].transpose(0, 2, 1)),
        "weights": lay(np.concatenate([pieces[n] for n in W_COLS], axis=1)),
        "vec_rows": lay(np.concatenate([vec[n] for n in ROWS])),
        "vec_cols": lay(np.stack([vec[n] for n in VECS], axis=1)),
    }
    nc = bacc.Bacc("TRN2", target_bir_lowering=False, num_devices=1)
    args = [nc.dram_tensor(n, arrays[n].shape, mybir.dt.from_np(arrays[n].dtype), kind="ExternalInput").ap()
            for n in _INPUTS]
    out = nc.dram_tensor("out", (GRAPHS, P, TILES * DIM), F32, kind="ExternalOutput").ap()
    build(nc, *args, out)
    got = run_bass_kernel_spmd(nc, [arrays], core_ids=[0]).results[0]["out"]
    return got.reshape(GRAPHS, P, TILES, DIM).transpose(0, 2, 1, 3).reshape(GRAPHS, NODES, DIM)
```

```python
from contextlib import ExitStack

import concourse.bass as bass
from concourse import mybir

ALU = mybir.AluOpType
ACT = mybir.ActivationFunctionType
F32 = mybir.dt.float32
F32R = mybir.dt.float32r
F16 = mybir.dt.float16
BF16 = mybir.dt.bfloat16
I32 = mybir.dt.int32

GRAPHS, NODES, DIM = 16, 512, 128
P = 128
TILES = NODES // P
HEADS = 8
HEAD = DIM // HEADS
GROUP = 4
GROUPS = HEADS // GROUP
SLOT = 32
DFF = 4 * DIM
FT = DFF // P
RELS = 4
RELATION = (2, 3, 4, 1)
EPS = 1e-5
SCALE = 1.0 / HEAD ** 0.5
NEVER = -1e30
NEG_BIG = -9e15
ALPHA = 0.2
UP = 4096.0
PACK = 64
ONE_ROW, SHIFT_ROW = PACK, PACK + 1

W_COLS = {}
_at = 0
for _n, _w in (("q", P), ("k", P), ("v", P), ("o", P), ("ff1", DFF), ("ff2", DFF), ("gat", P), ("gatT", P),
               ("rel", RELS * P), ("root1", P), ("near1", P), ("root2", P), ("near2", P), ("ident", P)):
    W_COLS[_n] = (_at, _at + _w)
    _at += _w
W_ALL = _at

VECS = ("bq", "bk", "bv", "bo", "g1", "b1", "g2", "b2", "ff1_0", "ff1_1", "ff1_2", "ff1_3", "ff2", "bias", "c1", "c2",
        "a_l", "a_r")
ROWS = ("bv", "bo", "g1", "b1", "g2", "b2", "ff2", "bias", "c1", "c2")

SCORE_TILES = HEADS * TILES


def order(text):
    return [(role, what, int(n)) for role, what, n in (piece.split(".") for piece in text.split())]


PE_ORDER = order("""
    attn.S.0 attn.S.1 attn.S.2 mid.V.7 late.agg.0 late.agg.1 mid.turn_ctx.0 attn.S.3 late.agg.2 late.agg.3 next.proj.0
    mid.turn_back.0 late.rel.0 attn.S.4 attn.S.5 mid.wo.0 late.agg.4 late.agg.5 attn.S.6 attn.S.7 next.proj.1
    late.rel.1 late.agg.6 late.agg.7 attn.S.8 attn.S.9 mid.turn_z.0 late.rel.2 attn.S.10 attn.S.11 mid.ff1.0 attn.S.12
    attn.S.13 mid.ff1.1 attn.S.14 late.rel.3 attn.S.15 mid.ff1.2 mid.ff1.3 attn.M.0 attn.S.16 attn.S.17 next.proj.2
    mid.ff2.0 mid.ff2.1 mid.ff2.2 mid.ff2.3 attn.T.0 attn.S.18 late.turn_y3.0 late.near1.0 attn.T.1 attn.S.19
    late.near1.1 attn.T.2 attn.S.20 attn.T.3 late.root.0 attn.S.21 late.near_w.0 attn.T.4 attn.S.22 attn.T.5 attn.S.23
    attn.V.0 attn.T.6 attn.S.24 attn.T.7 attn.S.25 attn.T.8 attn.V.1 mid.turn_y1.0 attn.S.26 attn.T.9 attn.S.27
    mid.gat_right.0 mid.gat_h.0 attn.T.10 attn.S.28 attn.T.11 mid.gat_h.1 late.turn_h1.0 late.near2.0 late.near2.1
    late.near2.2 attn.S.29 late.root.1 late.near_w.1 attn.T.12 attn.S.30 attn.T.13 attn.S.31 attn.V.2 attn.M.1
    attn.T.14 attn.T.15 mid.gat_turn.0 mid.gat_turn.1 attn.V.3 mid.gat_turn.2 mid.gat_turn.3 attn.T.16 attn.T.17
    attn.T.18 mid.gat_sum.0 mid.gat_sum.1 mid.gat_sum.2 mid.gat_sum.3 attn.T.19 attn.T.20 attn.T.21 attn.T.22
    attn.T.23 attn.T.24 attn.T.25 attn.V.4 attn.T.26 attn.T.27 attn.T.28 attn.V.5 attn.T.29 attn.T.30 attn.T.31
    attn.V.6
""")
ACT_ORDER = order("""
    mid.C.1 late.agg.0 mid.back.0 late.agg.1 next.proj.0 late.agg.2 next.proj.1 late.agg.3 mid.z.0 mid.ff1.0 mid.ff1.1
    mid.ff1.2 mid.ff1.3 attn.M.0 late.degree.0 late.high.0 attn.T.0 attn.T.1 late.y3.0 late.near.0 attn.T.2 attn.T.3
    attn.T.4 attn.T.5 attn.T.6 late.elu.0 attn.T.7 late.part.0 attn.T.8 mid.y1.0 late.part.1 attn.T.9 mid.h.0
    attn.T.10 attn.T.11 mid.h.1 late.h1.0 late.near.1 mid.gat_exp.0 mid.gat_exp.1 attn.T.12 mid.gat_exp.2 attn.T.13
    mid.gat_exp.3 attn.M.1 attn.T.14 attn.T.15 mid.gat_turn.0 mid.gat_turn.1 mid.gat_turn.2 mid.gat_turn.3 attn.C.0
    late.elu.1 attn.T.16 attn.T.17 attn.T.18 attn.T.19 attn.T.20 attn.T.21 attn.T.22 attn.T.23 attn.T.24 attn.T.25
    attn.T.26 attn.T.27 attn.T.28 mid.high.0 attn.T.29 attn.T.30 attn.T.31
""")
DVE_ORDER = order("""
    late.rel_mask.0 attn.S.0 late.is_one.0 late.rel_mask.1 late.rel_mask.2 mid.ctx.0 attn.S.1 attn.S.2 attn.S.3
    attn.S.4 late.rel_mask.3 next.proj.0 mid.resid.0 mid.stats.0 mid.moments.0 attn.S.5 attn.S.6 mid.apply.0 attn.S.7
    attn.S.8 attn.S.9 attn.S.10 attn.S.11 attn.S.12 attn.S.13 attn.S.14 late.resid.0 attn.S.15 next.proj.1
    late.stats.0 late.moments.0 attn.S.16 attn.S.17 late.apply.0 next.proj.2 late.degree.0 late.low.0 mid.resid.1
    mid.stats.1 mid.moments.1 attn.S.18 attn.S.19 mid.apply.1 attn.S.20 late.root.0 attn.S.21 late.pre.0 attn.S.22
    mid.stats.2 late.elu_low.0 mid.moments.2 attn.S.23 attn.S.24 late.elu.0 mid.apply.2 attn.S.25 late.part.0
    attn.S.26 attn.S.27 late.part.1 mid.gat_max.0 mid.gat_max.1 mid.gat_max.2 mid.gat_max.3 attn.S.28 mid.gat_top.0
    mid.gat_e.0 mid.gat_e.1 mid.gat_e.2 mid.gat_e.3 mid.leaky.0 mid.leaky.1 attn.S.29 mid.leaky.2 mid.leaky.3
    attn.S.30 attn.S.31 attn.no_edge.0 next.codes.0 late.root.1 late.pre.1 late.elu_low.1 late.elu.1 late.resid.1
    late.stats.1 late.moments.1 mid.gat_inv.0 mid.resid.3 mid.stats.3 mid.moments.3 late.apply.1 mid.apply.3
    next.codes.1 next.barred.0 mid.low.0 next.barred.1 next.barred.2
""")
POOL_ORDER = order("""
    mid.x.0 mid.rstd.0 late.rstd.0 mid.x1.0 mid.rstd.1 mid.y1.0 mid.rstd.2 late.rstd.1 mid.rstd.3 mid.y2.0
""")
SP_ORDER = order("""
    next.xT.0 next.adj.0 attn.pack.1 attn.M.0 next.bounce.0 next.bounce.1 mid.codes.0 mid.codesT.0 attn.x.0 attn.M.1
    next.pack.0 next.adjT.0 next.spill.0 late.store.0
""")
NORM = ("stats", "moments", "apply")


def build(nc, x, xT, adj, adjT, weights, vec_rows, vec_cols, out):
    with ExitStack() as ctx:
        def sb(name, shape, dt=F32):
            return ctx.enter_context(nc.sbuf_tensor(name, shape, dt))

        def sem(name):
            return ctx.enter_context(nc.semaphore(name))

        wts = sb("wts", [P, W_ALL])
        cols = sb("cols", [P, len(VECS)])
        rows = sb("rows", [P, len(ROWS), DIM])
        gat_ext = sb("gat_ext", [P, DIM + 1])
        gat_right = sb("gat_right", [P, P])
        a_right = sb("a_right", [P, P])
        ff_bias = sb("ff_bias", [P, DIM])
        not_self = sb("not_self", [P, P], BF16)
        ident16 = sb("ident16", [P, P], BF16)
        eps_tile = sb("eps_tile", [P, TILES])
        half_tile = sb("half_tile", [P, TILES])

        adj_in = sb("adj_in", [P, TILES, NODES], I32)
        codes = [sb(f"codes{i}", [P, TILES, NODES], BF16) for i in range(2)]
        codesT_late = sb("codesT_late", [P, TILES, NODES], BF16)
        barred = [sb(f"barred{i}", [P, TILES, NODES], BF16) for i in range(2)]
        x_nat = sb("x_nat", [P, TILES, DIM])
        x_turned = sb("x_turned", [P, NODES])
        q_hi = sb("q_hi", [P, NODES], F32R)
        q_lo = sb("q_lo", [P, NODES], F32R)
        k_hi = sb("k_hi", [P, NODES], F32R)
        k_lo = sb("k_lo", [P, NODES], F32R)
        q_pack = sb("q_pack", [SHIFT_ROW + 1, HEADS, NODES], F32R)
        k_pack = sb("k_pack", [SHIFT_ROW + 1, HEADS, NODES], F32R)
        values = [sb(f"values{i}", [P, TILES, HEADS, SLOT]) for i in range(2)]
        maxima = sb("maxima", [P, HEADS * TILES])
        shift = sb("shift", [GROUP * TILES, P], F32R)
        probs = [sb(f"probs{i}", [P, GROUP, NODES]) for i in range(4)]
        ctx_T = [sb(f"ctx_T{i}", [P, NODES]) for i in range(GROUPS)]

        ctx_sum = sb("ctx_sum", [P, TILES * HEADS])
        mid_T = [sb(f"mid_T{i}", [P, NODES]) for i in range(2)]
        late_T = [sb(f"late_T{i}", [P, NODES]) for i in range(2)]
        big_a = sb("big_a", [P, TILES, NODES])
        big_b = sb("big_b", [P, TILES, NODES])
        agg_T = [sb(f"agg_T{i}", [P, NODES]) for i in range(2)]
        x_bo_y1 = sb("x_bo_y1", [P, TILES, DIM])
        x1_y2 = sb("x1_y2", [P, TILES, DIM])
        x_b2 = sb("x_b2", [P, TILES, DIM])
        z_mid = sb("z_mid", [P, TILES, DIM])
        resid_mid = sb("resid_mid", [P, TILES, DIM])
        y2_rest = sb("y2_rest", [P, TILES, DIM])
        y3 = sb("y3", [P, TILES, DIM])
        pre = sb("pre", [P, TILES, DIM])
        act_out = sb("act_out", [P, TILES, DIM])
        resid_late = sb("resid_late", [P, TILES, DIM])
        stats = {r: sb(f"stats_{r}", [P, TILES, 6]) for r in ("mid", "late")}
        moments = {r: sb(f"moments_{r}", [P, TILES, 2]) for r in ("mid", "late")}
        spread = {r: sb(f"spread_{r}", [P, TILES]) for r in ("mid", "late")}
        rstd = {r: sb(f"rstd_{r}", [P, TILES]) for r in ("mid", "late")}
        no_edge = sb("no_edge", [P, TILES, NODES], BF16)
        is_one = sb("is_one", [P, TILES, NODES], BF16)
        is_rel = [sb(f"is_rel{i}", [P, TILES, NODES], F16) for i in range(2)]
        h_ext = sb("h_ext", [P, TILES, DIM + 1])
        gat_max = sb("gat_max", [P, TILES])
        gat_top = sb("gat_top", [P, TILES])
        gat_low = sb("gat_low", [P, TILES])
        gat_total = sb("gat_total", [P, TILES])
        gat_inv = sb("gat_inv", [P, TILES])
        degree = sb("degree", [P, TILES])
        deg_copy = [agg_T[t // 2][:, :].bitcast(F16)[:, (t % 2) * NODES:(t % 2 + 1) * NODES] for t in range(TILES)]
        deg_inv = sb("deg_inv", [P, TILES])
        part_hi = sb("part_hi", [P, TILES, DIM], F16)
        part_lo = sb("part_lo", [P, TILES, DIM], F16)
        h_parts = [is_rel[0][:, i, :].bitcast(BF16).rearrange("p (t c) -> p t c", t=TILES) for i in range(3)]

        RING = 3
        ring = [ctx.enter_context(nc.psum_tensor(f"ring{i}", [P, 512], F32)) for i in range(RING)]
        C_bank = ctx.enter_context(nc.psum_tensor("C_bank", [P, 512], F32))
        A_pair = ctx.enter_context(nc.psum_tensor("A_pair", [P, 2, 512], F32))
        A = [A_pair[:, 0, :], A_pair[:, 1, :]]
        B = [ctx.enter_context(nc.psum_tensor(f"B_bank{i}", [P, 512], F32))[:, :] for i in range(2)]

        bounce = [nc.dram_tensor(f"bounce{i}", [4, P, NODES], F32).ap() for i in range(2)]
        codes_dram = [nc.dram_tensor(f"codes_dram{i}", [GRAPHS, P, TILES * NODES], BF16).ap() for i in range(2)]

        def w(name, a=0, b=None):
            lo, hi = W_COLS[name]
            return wts[:, lo + a:(hi if b is None else lo + b)]

        def col(name):
            n = VECS.index(name)
            return cols[:, n:n + 1]

        def row4(name):
            return rows[:, ROWS.index(name):ROWS.index(name) + 1, :].broadcast_to((P, TILES, DIM))

        def nat(bank):
            return bank.rearrange("p (t c) -> p t c", t=TILES)

        qkv_in = sem("qkv_in")
        rows_in = sem("rows_in")
        weights_in = sem("weights_in")
        pack_consts = sem("pack_consts")
        values_zeroed = sem("values_zeroed")
        dve_consts = sem("dve_consts")
        pool_consts = sem("pool_consts")
        ff_bias_ready = sem("ff_bias_ready")
        gat_a_ready = sem("gat_a_ready")
        gat_w_psum = sem("gat_w_psum")
        gat_w_ready = sem("gat_w_ready")
        gate = sem("gate")
        adj_loaded = sem("adj_loaded")
        x_loaded = sem("x_loaded")
        xT_loaded = sem("xT_loaded")
        coded = sem("coded")
        spilled = sem("spilled")
        allow = sem("allow")
        no_edge_ready = sem("no_edge_ready")
        q_proj, k_proj, v_proj = sem("q_proj"), sem("k_proj"), sem("v_proj")
        qk_hi = sem("qk_hi")
        qk_lo = sem("qk_lo")
        v_ready = sem("v_ready")
        bounced = sem("bounced")
        packed = [sem(f"packed{i}") for i in range(GROUPS)]
        scored = sem("scored")
        maxed = sem("maxed")
        max_turned = sem("max_turned")
        shift_ready = sem("shift_ready")
        shift_packed = sem("shift_packed")
        shifted = sem("shifted")
        exped = sem("exped")
        weighted = sem("weighted")
        ctx_copied = sem("ctx_copied")
        resid_ready = {r: sem(f"resid_ready_{r}") for r in ("mid", "late")}
        stats_ready = {r: sem(f"stats_ready_{r}") for r in ("mid", "late")}
        moments_ready = {r: sem(f"moments_ready_{r}") for r in ("mid", "late")}
        spread_ready = {r: sem(f"spread_ready_{r}") for r in ("mid", "late")}
        rstd_ready = {r: sem(f"rstd_ready_{r}") for r in ("mid", "late")}
        normed = {r: sem(f"normed_{r}") for r in ("mid", "late")}
        ctx_turned = sem("ctx_turned")
        ctx_inv = sem("ctx_inv")
        ctx_scaled = sem("ctx_scaled")
        ctx_back = sem("ctx_back")
        ctx_back_in = sem("ctx_back_in")
        x_bo_ready = sem("x_bo_ready")
        x_b2_ready = sem("x_b2_ready")
        wo_done = sem("wo_done")
        z_turned = sem("z_turned")
        z_in = sem("z_in")
        z_scaled = sem("z_scaled")
        x1_ready = sem("x1_ready")
        ff1_done = sem("ff1_done")
        ff1_in = sem("ff1_in")
        ff2_done = sem("ff2_done")
        z2_scaled = sem("z2_scaled")
        y1_turned = sem("y1_turned")
        y1_in = sem("y1_in")
        gat_right_done = sem("gat_right_done")
        h_done = sem("h_done")
        h_in = sem("h_in")
        gat_maxed = sem("gat_maxed")
        gat_sum_max = sem("gat_sum_max")
        gat_top_ready = sem("gat_top_ready")
        gat_low_ready = sem("gat_low_ready")
        gat_e = sem("gat_e")
        gat_leaky = sem("gat_leaky")
        gat_exped = sem("gat_exped")
        gat_pT = sem("gat_pT")
        gat_pT_in = sem("gat_pT_in")
        gat_done = sem("gat_done")
        gat_inv_ready = sem("gat_inv_ready")
        hi_ready = sem("hi_ready")
        lo_ready = sem("lo_ready")
        y2_bias = sem("y2_bias")
        codesT_back = sem("codesT_back")
        codes_back = sem("codes_back")
        rel_mask = sem("rel_mask")
        agg_done = sem("agg_done")
        agg_in = sem("agg_in")
        rel_done = sem("rel_done")
        one_mask = sem("one_mask")
        y3_hi = sem("y3_hi")
        y3_lo = sem("y3_lo")
        y3_turned = sem("y3_turned")
        y3_in = sem("y3_in")
        near_done = sem("near_done")
        near_in = sem("near_in")
        deg_done = sem("deg_done")
        deg_ready = sem("deg_ready")
        deg_inv_ready = sem("deg_inv_ready")
        root_done = sem("root_done")
        near_w_done = sem("near_w_done")
        root_in = sem("root_in")
        pre_ready = sem("pre_ready")
        pre_low = sem("pre_low")
        pre_exp = sem("pre_exp")
        elu_ready = sem("elu_ready")
        part_ready = sem("part_ready")
        rest1 = sem("rest1")
        part3 = sem("part3")
        h1_turned = sem("h1_turned")
        h1_in = sem("h1_in")
        stored = sem("stored")

        def first(g):
            return isinstance(g, int) and g == 0

        def alone(eng, s, value):
            eng.wait_ge(s, value)
            eng.sem_inc(gate, 1)

        USES = [(what, n) for _, what, n in PE_ORDER if what in ("S", "T", "M")]

        def read_by(what, n):
            if what == "M":
                return shift_ready, GROUPS, n + 1
            return (maxed if what == "S" else exped), SCORE_TILES, n + 1

        def bank_of(what, n):
            return ring[USES.index((what, n)) % RING]

        def wait_bank(eng, g, what, n):
            u = USES.index((what, n)) - RING
            if u < 0 and first(g):
                return
            signal, per, count = read_by(*USES[u % len(USES)])
            eng.wait_ge(signal, g * per + (count - (per if u < 0 else 0)))

        def steps(eng, order, piece):
            def step(i, parity, roles):
                graph = {"next": (i + 1, 1 - parity), "attn": (i, parity), "mid": (i - 1, 1 - parity),
                         "late": (i - 2, parity)}
                for role, what, n in order:
                    if role in roles:
                        piece(role, *graph[role], what, n)

            step(0, 0, ("next", "attn"))
            step(1, 1, ("next", "attn", "mid"))
            step(2, 0, ("next", "attn", "mid", "late"))
            with eng.Fori(0, (GRAPHS - 4) // 2) as n:
                step(n * 2 + 3, 1, ("next", "attn", "mid", "late"))
                step(n * 2 + 4, 0, ("next", "attn", "mid", "late"))
            step(GRAPHS - 1, 1, ("attn", "mid", "late"))
            step(GRAPHS, 0, ("mid", "late"))
            step(GRAPHS + 1, 1, ("late",))

        block = ctx.enter_context(nc.Block())

        @block.sync
        def _(sp):
            qkv = W_COLS["v"][1]
            sp.dma_start(wts[:, 0:qkv], weights[:, 0:qkv]).then_inc(qkv_in, 16)
            sp.dma_start(x_turned[:, :], xT[0]).then_inc(xT_loaded, 16)
            sp.dma_start(cols[:, :], vec_cols).then_inc(qkv_in, 16)
            sp.dma_start(adj_in[:, :, :].rearrange("p t n -> p (t n)"), adj[0]).then_inc(adj_loaded, 16)
            sp.dma_start(rows[:, :, :].rearrange("p a b -> p (a b)"),
                         vec_rows.partition_broadcast(P)).then_inc(rows_in, 16)
            sp.dma_start(wts[:, qkv:], weights[:, qkv:]).then_inc(weights_in, 16)

            def flat(t):
                return t.rearrange("p t n -> p (t n)")

            def piece(role, g, p, what, n):
                if what == "x":
                    if not first(g):
                        sp.wait_ge(x_bo_ready, g)
                        sp.wait_ge(x_b2_ready, g)
                    sp.dma_start(flat(x_nat[:, :, :]), x[g]).then_inc(x_loaded, 16)
                if what == "xT":
                    if not first(g):
                        sp.wait_ge(v_proj, g)
                    sp.dma_start(x_turned[:, :], xT[g]).then_inc(xT_loaded, 16)
                if what == "adj":
                    if not first(g):
                        sp.wait_ge(coded, g * 2)
                    sp.dma_start(flat(adj_in[:, :, :]), adj[g]).then_inc(adj_loaded, 16)
                if what == "adjT":
                    sp.wait_ge(coded, g * 2 + 1)
                    sp.dma_start(flat(adj_in[:, :, :]), adjT[g]).then_inc(adj_loaded, 16)
                    sp.dma_start(codes_dram[0][g], flat(codes[0][:, :, :])).then_inc(spilled, 16)
                if what == "spill":
                    sp.wait_ge(coded, g * 2 + 2)
                    sp.dma_start(codes_dram[1][g], flat(codes[1][:, :, :])).then_inc(spilled, 16)
                if what == "codesT":
                    alone(sp, spilled, g * 32 + 32)
                    if not first(g):
                        sp.wait_ge(rel_mask, g * 4)
                    sp.dma_start(flat(codesT_late[:, :, :]), codes_dram[1][g]).then_inc(codesT_back, 16)
                if what == "codes":
                    if not first(g):
                        sp.wait_ge(near_done, g * 2)
                    sp.dma_start(flat(is_one[:, :, :]), codes_dram[0][g]).then_inc(codes_back, 16)
                if what == "bounce":
                    for s, src in ((qk_hi, (q_hi, k_hi)[n]), (qk_lo, (q_lo, k_lo)[n])):
                        sp.wait_ge(s, g * 2 + (n + 1))
                        sp.dma_start(bounce[p][2 * n + (s is qk_lo)], src[:, :].bitcast(F32)).then_inc(bounced, 16)
                if what == "pack":
                    alone(sp, bounced, g * 64 + 64)
                    if not first(g):
                        sp.wait_ge(shifted, g * 32 + (16 * (n + 1) - 32))
                    for dst, parts in ((q_pack, (0, 0, 1, 1)), (k_pack, (2, 3, 2, 3))):
                        for b, part in enumerate(parts):
                            src = bounce[p][part].rearrange("(h d) n -> d h n", h=HEADS)
                            sp.dma_start(dst[b * HEAD:(b + 1) * HEAD, n * GROUP:(n + 1) * GROUP, :].bitcast(F32),
                                         src[:, n * GROUP:(n + 1) * GROUP, :]).then_inc(packed[n], 16)
                if what == "M":
                    sp.wait_ge(shift_ready, g * 2 + (n + 1))
                    sp.dma_start(q_pack[SHIFT_ROW:SHIFT_ROW + 1, n * GROUP:(n + 1) * GROUP, :]
                                 .rearrange("o h (t q) -> o (h t) q", t=TILES).bitcast(F32),
                                 shift[:, :].bitcast(F32)).then_inc(shift_packed, 16)
                if what == "store":
                    sp.wait_ge(normed["late"], g * 2 + 2)
                    sp.dma_start(out[g], flat(resid_late[:, :, :])).then_inc(stored, 16)

            for what, n in (("bounce", 0), ("bounce", 1), ("adjT", 0)):
                piece("next", 0, 0, what, n)
            sp.wait_ge(pack_consts, 2)
            piece("next", 0, 0, "pack", 0)
            piece("next", 0, 0, "spill", 0)
            steps(sp, SP_ORDER, piece)
            sp.wait_ge(stored, 16 * GRAPHS)
            sp.wait_ge(spilled, 32 * GRAPHS)
            sp.wait_ge(bounced, 64 * GRAPHS)

        @block.tensor
        def _(pe):
            ident = w("ident")

            def turn(dst, src):
                for t in range(TILES):
                    last = nc.tensor.transpose(dst[:, t * P:(t + 1) * P], src[:, t, :], ident)
                return last

            def apply_w(dst, srcT, wt):
                for t in range(TILES):
                    last = nc.tensor.matmul(nat(dst)[:, t, :], srcT[:, t * P:(t + 1) * P], wt, start=True, stop=True)
                return last

            def project(g, n):
                if n == 0:
                    pe.wait_ge(xT_loaded, g * 16 + 16)
                    if not (isinstance(g, int) and g < 2):
                        pe.wait_ge(ctx_copied, g * 2 - 2)
                    nc.tensor.matmul(C_bank[:, :], w("q"), x_turned[:, :], start=True, stop=True).then_inc(q_proj, 1)
                if n == 1:
                    pe.wait_ge(qk_lo, g * 2 + 1)
                    nc.tensor.matmul(C_bank[:, :], w("k"), x_turned[:, :], start=True, stop=True).then_inc(k_proj, 1)
                if n == 2:
                    pe.wait_ge(qk_lo, g * 2 + 2)
                    apply_w(C_bank[:, :], x_turned, w("v")).then_inc(v_proj, 1)

            def attention(g, p, what, n):
                if what == "S":
                    h, t = divmod(n, TILES)
                    if n % (GROUP * TILES) == 0:
                        pe.wait_ge(packed[h // GROUP], g * 128 + 128)
                    wait_bank(pe, g, "S", n)
                    nc.tensor.matmul(bank_of("S", n)[:, :], q_pack[0:ONE_ROW + 1, h, t * P:(t + 1) * P],
                                     k_pack[0:ONE_ROW + 1, h, :], start=True, stop=True).then_inc(scored, 1)
                if what == "M":
                    pe.wait_ge(maxed, g * 32 + 16 * (n + 1))
                    wait_bank(pe, g, "M", n)
                    nc.tensor.transpose(bank_of("M", n)[0:GROUP * TILES, 0:P], maxima[:, n * 16:(n + 1) * 16],
                                        ident).then_inc(max_turned, 1)
                if what == "T":
                    slot, j = divmod(n, GROUP)
                    grp, kt = divmod(slot, TILES)
                    h = grp * GROUP + j
                    if kt == 0 and j == 0:
                        pe.wait_ge(shift_packed, g * 32 + 16 * (grp + 1))
                        if grp == 0:
                            pe.wait_ge(allow, g * 3 + 3)
                    wait_bank(pe, g, "T", n)
                    nc.tensor.matmul(bank_of("T", n)[:, :], k_pack[:, h, kt * P:(kt + 1) * P], q_pack[:, h, :],
                                     start=True, stop=False)
                    nc.tensor.matmul(bank_of("T", n)[:, :], ident16[:, :], barred[p][:, kt, :], start=False,
                                     stop=True).then_inc(shifted, 1)
                if what == "V":
                    grp, kt = divmod(n, TILES)
                    if n == 0:
                        if isinstance(g, int) and g == GRAPHS - 1:
                            pe.wait_ge(v_ready, GRAPHS)
                            pe.wait_ge(ctx_copied, 2 * g)
                        else:
                            pe.wait_ge(v_ready, g + 2)
                    if n == TILES:
                        pe.wait_ge(ctx_copied, g * 2 + 1)
                    pe.wait_ge(exped, g * SCORE_TILES + GROUP * (n + 1))
                    for j in range(GROUP):
                        last = nc.tensor.matmul(C_bank[j * SLOT:(j + 1) * SLOT, :],
                                                values[p][:, kt, grp * GROUP + j, :], probs[n % 4][:, j, :],
                                                start=(kt == 0), stop=(kt == TILES - 1),
                                                tile_position=(0, j * SLOT))
                    last.then_inc(weighted, 1)

            def mid(g, p, what, n):
                if what == "turn_ctx":
                    pe.wait_ge(ctx_copied, g * 2 + 2)
                    if not first(g):
                        pe.wait_ge(resid_ready["mid"], g * 4)
                    for t in range(TILES):
                        for grp in range(GROUPS):
                            c = (t % 2) * 256 + grp * P
                            last = nc.tensor.transpose(A_pair[:, t // 2, c:c + P], ctx_T[grp][:, t * P:(t + 1) * P], ident)
                    last.then_inc(ctx_turned, 1)
                if what == "turn_back":
                    pe.wait_ge(ctx_scaled, g + 1)
                    turn(A[0], z_mid).then_inc(ctx_back, 1)
                if what == "wo":
                    pe.wait_ge(ctx_back_in, g + 1)
                    apply_w(A[1], mid_T[0], w("o")).then_inc(wo_done, 1)
                if what == "turn_z":
                    pe.wait_ge(normed["mid"], g * 4 + 1)
                    turn(A[0], z_mid).then_inc(z_turned, 1)
                if what == "ff1":
                    if n == 0:
                        pe.wait_ge(z_in, g + 1)
                    if n >= 2:
                        pe.wait_ge(ff1_in, g * 4 + (n - 1))
                    nc.tensor.matmul(A[(n + 1) % 2], w("ff1", n * P, (n + 1) * P), mid_T[1][:, :],
                                     start=True, stop=True).then_inc(ff1_done, 1)
                if what == "ff2":
                    if n == 0:
                        pe.wait_ge(ff1_in, g * 4 + 4)
                    for f in range(FT):
                        last = nc.tensor.matmul(nat(A[1])[:, n, :], big_a[:, f, n * P:(n + 1) * P],
                                                w("ff2", f * P, (f + 1) * P), start=(f == 0), stop=(f == FT - 1))
                    if n == TILES - 1:
                        last.then_inc(ff2_done, 1)
                if what == "turn_y1":
                    pe.wait_ge(normed["mid"], g * 4 + 3)
                    turn(A[0], x_bo_y1).then_inc(y1_turned, 1)
                if what == "gat_right":
                    pe.wait_ge(y1_in, g + 1)
                    nc.tensor.matmul(A[1], gat_right[:, :], mid_T[0][:, :], start=True,
                                     stop=True).then_inc(gat_right_done, 1)
                if what == "gat_h":
                    if n == 1:
                        pe.wait_ge(h_in, g * 2 + 1)
                    for t in (2 * n, 2 * n + 1):
                        c = (t % 2) * 256
                        last = nc.tensor.matmul(A[0][:, c:c + DIM + 1], mid_T[0][:, t * P:(t + 1) * P],
                                                gat_ext[:, :], start=True, stop=True)
                    last.then_inc(h_done, 1)
                if what == "gat_turn":
                    if n == 0:
                        pe.wait_ge(gat_exped, g * 4 + 4)
                    if n >= 2:
                        pe.wait_ge(gat_pT_in, g * 4 + (n - 1))
                    for it in range(TILES):
                        last = nc.tensor.transpose(A[n % 2][:, it * P:(it + 1) * P],
                                                   big_b[:, it, n * P:(n + 1) * P], ident)
                    last.then_inc(gat_pT, 1)
                if what == "gat_sum":
                    if n == 0:
                        pe.wait_ge(gat_pT_in, g * 4 + 4)
                    for jt in range(TILES):
                        last = nc.tensor.matmul(nat(A[0])[:, n, :], big_a[:, jt, n * P:(n + 1) * P],
                                                h_ext[:, jt, 0:DIM], start=(jt == 0), stop=(jt == TILES - 1))
                    if n == TILES - 1:
                        last.then_inc(gat_done, 1)

            def late(g, p, what, n):
                if what == "agg":
                    r, half = divmod(n, 2)
                    if half == 0:
                        if r == 0:
                            pe.wait_ge(lo_ready, g + 1)
                            if not first(g):
                                pe.wait_ge(pre_ready, g * 2)
                        else:
                            pe.wait_ge(agg_in, g * 4 + r)
                        pe.wait_ge(rel_mask, g * 4 + (r + 1))
                    for mt in (2 * half, 2 * half + 1):
                        for k, part in enumerate((part_hi, part_lo)):
                            last = nc.tensor.matmul(B[0], part[:, mt, :], is_rel[r % 2][:, mt, :],
                                                    start=(mt == 0 and k == 0), stop=(mt == TILES - 1 and k == 1))
                    if half == 1:
                        last.then_inc(agg_done, 1)
                if what == "rel":
                    pe.wait_ge(agg_in, g * 4 + (n + 1))
                    for t in range(TILES):
                        last = nc.tensor.matmul(nat(B[1])[:, t, :], agg_T[n % 2][:, t * P:(t + 1) * P],
                                                w("rel", (RELATION[n] - 1) * P, RELATION[n] * P), start=(n == 0 and t == 0),
                                                stop=(n == RELS - 1), skip_group_check=True)
                    last.then_inc(rel_done, 1)
                if what == "turn_y3":
                    pe.wait_ge(normed["late"], g * 2 + 1)
                    turn(B[0], y3).then_inc(y3_turned, 1)
                if what == "near1":
                    if n == 0:
                        pe.wait_ge(y3_lo, g + 1)
                        pe.wait_ge(one_mask, g + 1)
                    for it in (2 * n, 2 * n + 1):
                        for k, part in enumerate((part_hi, part_lo)):
                            last = nc.tensor.matmul(B[1], part[:, it, :], is_one[:, it, :],
                                                    start=(it == 0 and k == 0), stop=(it == TILES - 1 and k == 1))
                    if n == 1:
                        last.then_inc(near_done, 1)
                if what == "root":
                    pe.wait_ge(near_in if n == 0 else h1_in, g * (2 - n) + 1)
                    apply_w(B[1], late_T[0], w(("root1", "root2")[n])).then_inc(root_done, 1)
                if what == "near_w":
                    if n == 0:
                        pe.wait_ge(y3_in, g + 1)
                    else:
                        pe.wait_ge(near_in, g * 2 + 2)
                    apply_w(B[0], late_T[1], w(("near1", "near2")[n])).then_inc(near_w_done, 1)
                if what == "turn_h1":
                    pe.wait_ge(elu_ready, g * 2 + 1)
                    turn(B[1], act_out).then_inc(h1_turned, 1)
                if what == "near2":
                    if n == 0:
                        pe.wait_ge(part_ready, g * 2 + 1)
                    if n == 1:
                        pe.wait_ge(part_ready, g * 2 + 2)
                    if n == 2:
                        pe.wait_ge(part3, g + 1)
                    for it in range(TILES):
                        last = nc.tensor.matmul(B[0], h_parts[n][:, it, :], is_one[:, it, :],
                                                start=(it == 0 and n == 0), stop=(it == TILES - 1 and n == 2))
                    if n == 2:
                        last.then_inc(near_done, 1)

            def piece(role, g, p, what, n):
                if role == "next":
                    project(g, n)
                elif role == "attn" or what == "V":
                    attention(g, p, what, n)
                elif role == "mid":
                    mid(g, p, what, n)
                else:
                    late(g, p, what, n)

            pe.wait_ge(qkv_in, 32)
            for n in range(3):
                project(0, n)
            pe.wait_ge(weights_in, 16)
            pe.wait_ge(gat_a_ready, 1)
            nc.tensor.matmul(A[1][:, 0:P], w("gatT"), a_right[:, :], start=True, stop=True)
            nc.tensor.matmul(A[1][:, P:P + 1], w("gatT"), col("a_l"), start=True, stop=True).then_inc(gat_w_psum, 1)
            pe.wait_ge(dve_consts, 2)
            pe.wait_ge(gat_w_ready, 1)
            steps(pe, PE_ORDER, piece)

        @block.scalar
        def _(act):
            def piece(role, g, p, what, n):
                if what == "proj":
                    if n == 0 and not first(g):
                        act.wait_ge(bounced, g * 64)
                    act.wait_ge((q_proj, k_proj)[n], g + 1)
                    nc.scalar.activation((q_hi, k_hi)[n][:, :], C_bank[:, :], ACT.Identity,
                                         bias=col(("bq", "bk")[n])).then_inc(qk_hi, 1)
                if what == "M":
                    act.wait_ge(max_turned, g * 2 + (n + 1))
                    if not (first(g) and n == 0):
                        act.wait_ge(shift_packed, g * 32 + 16 * n)
                    nc.scalar.activation(shift[:, :], bank_of("M", n)[0:GROUP * TILES, 0:P], ACT.Copy,
                                         scale=-1.0).then_inc(shift_ready, 1)
                if what == "T":
                    slot, j = divmod(n, GROUP)
                    if j == 0 and not (first(g) and slot < 4):
                        act.wait_ge(weighted, g * 8 + (slot - 3))
                    act.wait_ge(shifted, g * 32 + (n + 1))
                    nc.scalar.activation(probs[slot % 4][:, j, :], bank_of("T", n)[:, :], ACT.Exp,
                                         scale=SCALE).then_inc(exped, 1)
                if what == "C":
                    act.wait_ge(weighted, g * 8 + 4 * (n + 1))
                    if not first(g):
                        act.wait_ge(ctx_turned, g)
                    nc.scalar.activation(ctx_T[n][:, :], C_bank[:, :], ACT.Copy).then_inc(ctx_copied, 1)
                if what == "back":
                    act.wait_ge(ctx_back, g + 1)
                    nc.scalar.activation(mid_T[0][:, :], A[0], ACT.Copy).then_inc(ctx_back_in, 1)
                if what == "z":
                    act.wait_ge(z_turned, g + 1)
                    nc.scalar.activation(mid_T[1][:, :], A[0], ACT.Identity, bias=col("b1"),
                                         scale=col("g1")).then_inc(z_in, 1)
                if what == "ff1":
                    act.wait_ge(ff1_done, g * 4 + (n + 1))
                    nc.scalar.activation(big_a[:, n, :], A[(n + 1) % 2], ACT.Relu, bias=col(f"ff1_{n}")).then_inc(ff1_in, 1)
                if what == "y1":
                    act.wait_ge(y1_turned, g + 1)
                    nc.scalar.activation(mid_T[0][:, :], A[0], ACT.Copy).then_inc(y1_in, 1)
                if what == "h":
                    act.wait_ge(h_done, g * 2 + (n + 1))
                    nc.scalar.activation(h_ext[:, 2 * n:2 * n + 2, :],
                                         A[0].rearrange("p (t c) -> p t c", t=2)[:, :, 0:DIM + 1],
                                         ACT.Copy).then_inc(h_in, 1)
                if what == "gat_exp":
                    if n == 0:
                        act.wait_ge(gat_low_ready, g + 1)
                    act.wait_ge(gat_leaky, g * 4 + (n + 1))
                    nc.scalar.activation(big_b[:, n, :], big_b[:, n, :], ACT.Exp, bias=gat_low[:, n:n + 1],
                                         accum_out=gat_total[:, n:n + 1]).then_inc(gat_exped, 1)
                if what == "gat_turn":
                    act.wait_ge(gat_pT, g * 4 + (n + 1))
                    nc.scalar.activation(big_a[:, n, :], A[n % 2], ACT.Copy).then_inc(gat_pT_in, 1)
                if what == "high":
                    if role == "mid":
                        act.wait_ge(normed["mid"], g * 4 + 4)
                        if not first(g):
                            act.wait_ge(near_done, g * 2 - 1)
                        nc.scalar.activation(part_hi[:, :, :], x1_y2[:, :, :], ACT.Copy, scale=UP).then_inc(hi_ready, 1)
                    else:
                        act.wait_ge(normed["late"], g * 2 + 1)
                        nc.scalar.activation(part_hi[:, :, :], y3[:, :, :], ACT.Copy, scale=UP).then_inc(y3_hi, 1)
                if what == "degree":
                    act.wait_ge(rel_mask, g * 4 + 4)
                    act.wait_ge(rel_done, g * 4 + 4)
                    if not first(g):
                        act.wait_ge(deg_ready, g)
                    for t in range(TILES):
                        last = nc.scalar.activation(deg_copy[t], is_rel[1][:, t, :], ACT.Copy,
                                                    accum_out=degree[:, t:t + 1])
                    last.then_inc(deg_done, 1)
                if what == "agg":
                    act.wait_ge(agg_done, g * 4 + (n + 1))
                    if n < 2 and not first(g):
                        act.wait_ge(deg_done, g)
                    if n >= 2:
                        act.wait_ge(rel_done, g * 4 + (n - 1))
                    nc.scalar.activation(agg_T[n % 2][:, :], B[0], ACT.Copy, scale=1.0 / UP).then_inc(agg_in, 1)
                if what == "y3":
                    act.wait_ge(y3_turned, g + 1)
                    nc.scalar.activation(late_T[0][:, :], B[0], ACT.Copy).then_inc(y3_in, 1)
                if what == "near":
                    act.wait_ge(near_done, g * 2 + (n + 1))
                    nc.scalar.activation(late_T[1][:, :], B[1 - n], ACT.Copy, scale=(1.0 / UP, 1.0)[n]).then_inc(near_in, 1)
                if what == "elu":
                    act.wait_ge(pre_low, g * 2 + (n + 1))
                    nc.scalar.activation(act_out[:, :, :], act_out[:, :, :], ACT.Exp).then_inc(pre_exp, 1)
                if what == "part":
                    if n == 0:
                        act.wait_ge(elu_ready, g * 2 + 1)
                        nc.scalar.activation(h_parts[0], act_out[:, :, :], ACT.Copy).then_inc(part_ready, 1)
                    else:
                        act.wait_ge(rest1, g + 1)
                        nc.scalar.activation(h_parts[1], y2_rest[:, :, :], ACT.Copy).then_inc(part_ready, 1)
                if what == "h1":
                    act.wait_ge(h1_turned, g + 1)
                    nc.scalar.activation(late_T[0][:, :], B[1], ACT.Copy).then_inc(h1_in, 1)

            act.wait_ge(qkv_in, 32)
            for n in range(2):
                piece("next", 0, 0, "proj", n)
            act.wait_ge(weights_in, 16)
            act.wait_ge(gat_w_psum, 1)
            nc.scalar.activation(gat_right[:, :], A[1][:, 0:P], ACT.Copy)
            nc.scalar.activation(gat_ext[:, 0:DIM], w("gat"), ACT.Copy)
            nc.scalar.activation(gat_ext[:, DIM:DIM + 1], A[1][:, P:P + 1], ACT.Copy).then_inc(gat_w_ready, 1)
            steps(act, ACT_ORDER, piece)

        @block.vector
        def _(dve):
            for p in range(2):
                nc.vector.memset(values[p][:, :, :, :], 0.0).then_inc(values_zeroed, 1)
            dve.wait_ge(values_zeroed, 2)
            for p in range(2):
                nc.vector.memset(values[p][:, :, :, HEAD:HEAD + 1], 1.0).then_inc(values_zeroed, 1)
            dve.wait_ge(qkv_in, 32)

            def next_graph(g, p, what, n):
                if what == "codes":
                    dve.wait_ge(adj_loaded, g * 32 + 16 * (n + 1))
                    if not first(g):
                        dve.wait_ge(spilled, g * 32 + (16 * (n + 1) - 32))
                        dve.wait_ge(allow, g * 3)
                        dve.wait_ge(no_edge_ready, g)
                    nc.vector.tensor_scalar(codes[n][:, :, :], adj_in[:, :, :], 0.0, RELS + 1.0, ALU.max,
                                            ALU.min).then_inc(coded, 1)
                if what == "no_edge":
                    dve.wait_ge(coded, g * 2 + 1)
                    if not first(g):
                        dve.wait_ge(gat_maxed, g * 4)
                    nc.vector.tensor_scalar(no_edge[:, :, :], codes[0][:, :, :], 0.5, NEG_BIG / ALPHA, ALU.is_lt,
                                            ALU.mult).then_inc(no_edge_ready, 1)
                if what == "barred" and n == 0:
                    dve.wait_ge(coded, g * 2 + 2)
                    if not (isinstance(g, int) and g < 2):
                        dve.wait_ge(shifted, g * 32 - 32)
                    nc.vector.tensor_tensor(barred[p][:, :, :], codes[0][:, :, :], codes[1][:, :, :],
                                            ALU.max).then_inc(allow, 1)
                if what == "barred" and n == 1:
                    dve.wait_ge(allow, g * 3 + 1)
                    nc.vector.tensor_scalar(barred[p][:, :, :], barred[p][:, :, :], 0.5, NEVER, ALU.is_lt,
                                            ALU.mult).then_inc(allow, 1)
                if what == "barred" and n == 2:
                    dve.wait_ge(allow, g * 3 + 2)
                    for t in range(TILES):
                        d = barred[p][:, t, t * P:(t + 1) * P]
                        last = nc.vector.tensor_tensor(d, d, not_self[:, :], ALU.mult)
                    last.then_inc(allow, 1)
                if what == "proj" and n < 2:
                    dve.wait_ge(qk_hi, g * 2 + (n + 1))
                    if n == 0 and not first(g):
                        dve.wait_ge(bounced, g * 64)
                    nc.vector.scalar_tensor_tensor((q_lo, k_lo)[n][:, :], C_bank[:, :], col(("bq", "bk")[n]),
                                                   (q_hi, k_hi)[n][:, :].bitcast(F32), ALU.add,
                                                   ALU.subtract).then_inc(qk_lo, 1)
                if what == "proj" and n == 2:
                    dve.wait_ge(v_proj, g + 1)
                    nc.vector.tensor_tensor(
                        values[p][:, :, :, 0:HEAD], C_bank[:, :].rearrange("p (t h d) -> p t h d", t=TILES, h=HEADS),
                        rows[:, 0:1, :].rearrange("p o (h d) -> p o h d", h=HEADS)
                        .broadcast_to((P, TILES, HEADS, HEAD)), ALU.add).then_inc(v_ready, 1)

            def attention(g, p, what, n):
                if what == "S":
                    if n == 0:
                        dve.wait_ge(allow, g * 3 + 3)
                    alone(dve, scored, g * 32 + (n + 1))
                    bank = bank_of("S", n)[:, :]
                    nc.vector.tensor_tensor_reduce(
                        out=bank, in0=bank, in1=barred[p][:, n % TILES, :], scale=1.0, scalar=-3e38, op0=ALU.add,
                        op1=ALU.max, accum_out=maxima[:, n:n + 1]).then_inc(maxed, 1)

            SOURCE = {"mid": resid_mid, "late": resid_late}
            RESULT = {"mid": (z_mid, z_mid, x_bo_y1, x1_y2), "late": (y3, resid_late)}

            def normalise(role, g, what, k):
                per, src, dst = len(RESULT[role]), SOURCE[role], RESULT[role][k]
                if what == "stats":
                    dve.wait_ge(resid_ready[role], g * per + (k + 1))
                    for t in range(TILES):
                        last = nc.vector.bn_stats(stats[role][:, t, :], src[:, t, :])
                    last.then_inc(stats_ready[role], 1)
                if what == "moments":
                    alone(dve, stats_ready[role], g * per + (k + 1))
                    for t in range(TILES):
                        last = nc.vector.bn_aggr(moments[role][:, t, :], stats[role][:, t, :])
                    last.then_inc(moments_ready[role], 1)
                if what == "apply":
                    dve.wait_ge(rstd_ready[role], g * per + (k + 1))
                    for t in range(TILES):
                        last = nc.vector.tensor_scalar(dst[:, t, :], src[:, t, :], moments[role][:, t, 0:1],
                                                       rstd[role][:, t:t + 1], ALU.subtract, ALU.mult)
                    last.then_inc(normed[role], 1)

            def mid(g, p, what, n):
                if what == "ctx":
                    dve.wait_ge(ctx_turned, g + 1)
                    src = A_pair[:, :, :].rearrange("p b (s d) -> p (b s) d", d=SLOT)
                    nc.vector.reciprocal(ctx_sum[:, :].rearrange("p (s o) -> p s o", o=1),
                                         src[:, :, HEAD:HEAD + 1]).then_inc(ctx_inv, 1)
                    dve.wait_ge(ctx_inv, g + 1)
                    nc.vector.tensor_tensor(
                        z_mid[:, :, :].rearrange("p t (h d) -> p (t h) d", h=HEADS), src[:, :, 0:HEAD],
                        ctx_sum[:, :].rearrange("p (s o) -> p s o", o=1).broadcast_to((P, TILES * HEADS, HEAD)),
                        ALU.mult).then_inc(ctx_scaled, 1)
                if what == "resid" and n == 0:
                    dve.wait_ge(wo_done, g + 1)
                    dve.wait_ge(x_bo_ready, g + 1)
                    nc.vector.tensor_tensor(resid_mid[:, :, :], nat(A[1]), x_bo_y1[:, :, :],
                                            ALU.add).then_inc(resid_ready["mid"], 1)
                if what == "resid" and n == 1:
                    dve.wait_ge(ff2_done, g + 1)
                    dve.wait_ge(x1_ready, g + 1)
                    nc.vector.tensor_tensor(resid_mid[:, :, :], nat(A[1]), x1_y2[:, :, :],
                                            ALU.add).then_inc(resid_ready["mid"], 1)
                if what == "gat_max":
                    if n == 0:
                        dve.wait_ge(gat_right_done, g + 1)
                        alone(dve, no_edge_ready, g + 1)
                    nc.vector.tensor_tensor_reduce(
                        out=big_b[:, n, :], in0=A[1], in1=no_edge[:, n, :], scale=1.0, scalar=-3e38,
                        op0=ALU.add, op1=ALU.max, accum_out=gat_max[:, n:n + 1]).then_inc(gat_maxed, 1)
                if what == "gat_top":
                    dve.wait_ge(gat_maxed, g * 4 + 4)
                    dve.wait_ge(h_in, g * 2 + 2)
                    m = gat_max[:, :].rearrange("p (t o) -> p t o", o=1)
                    nc.vector.tensor_tensor(m, m, h_ext[:, :, DIM:DIM + 1], ALU.add).then_inc(gat_sum_max, 1)
                if what == "gat_e":
                    nc.vector.tensor_scalar(big_b[:, n, :], big_b[:, n, :], h_ext[:, n, DIM:DIM + 1], None,
                                            ALU.add).then_inc(gat_e, 1)
                    if n == 0:
                        dve.wait_ge(gat_sum_max, g + 1)
                        nc.vector.scalar_tensor_tensor(gat_top[:, :], gat_max[:, :], ALPHA, gat_max[:, :], ALU.mult,
                                                       ALU.max).then_inc(gat_top_ready, 1)
                    if n == 1:
                        dve.wait_ge(gat_top_ready, g + 1)
                        nc.vector.tensor_scalar(gat_low[:, :], gat_top[:, :], -1.0, None,
                                                ALU.mult).then_inc(gat_low_ready, 1)
                if what == "leaky":
                    dve.wait_ge(gat_e, g * 4 + (n + 1))
                    nc.vector.scalar_tensor_tensor(big_b[:, n, :], big_b[:, n, :], ALPHA, big_b[:, n, :], ALU.mult,
                                                   ALU.max).then_inc(gat_leaky, 1)
                if what == "gat_inv":
                    dve.wait_ge(gat_exped, g * 4 + 4)
                    nc.vector.reciprocal(gat_inv[:, :], gat_total[:, :]).then_inc(gat_inv_ready, 1)
                if what == "resid" and n == 3:
                    dve.wait_ge(gat_inv_ready, g + 1)
                    dve.wait_ge(gat_done, g + 1)
                    for t in range(TILES):
                        last = nc.vector.scalar_tensor_tensor(resid_mid[:, t, :], nat(A[0])[:, t, :],
                                                              gat_inv[:, t:t + 1], x_bo_y1[:, t, :], ALU.mult, ALU.add)
                    last.then_inc(resid_ready["mid"], 1)
                if what == "low":
                    dve.wait_ge(hi_ready, g + 1)
                    nc.vector.scalar_tensor_tensor(part_lo[:, :, :], x1_y2[:, :, :], UP, part_hi[:, :, :], ALU.mult,
                                                   ALU.subtract).then_inc(lo_ready, 1)

            def late(g, p, what, n):
                if what == "rel_mask":
                    if n == 0:
                        dve.wait_ge(codesT_back, g * 16 + 16)
                        if not first(g):
                            dve.wait_ge(near_done, g * 2)
                    if not (first(g) and n < 2):
                        dve.wait_ge(agg_done, g * 4 + (n - 1))
                    if n == 1 and not first(g):
                        dve.wait_ge(deg_done, g)
                    nc.vector.tensor_scalar(is_rel[n % 2][:, :, :], codesT_late[:, :, :], float(RELATION[n]), None,
                                            ALU.is_equal).then_inc(rel_mask, 1)
                if what == "is_one":
                    dve.wait_ge(codes_back, g * 16 + 16)
                    nc.vector.tensor_scalar(is_one[:, :, :], is_one[:, :, :], 1.0, None,
                                            ALU.is_equal).then_inc(one_mask, 1)
                if what == "resid" and n == 0:
                    dve.wait_ge(rel_done, g * 4 + 4)
                    dve.wait_ge(y2_bias, g + 1)
                    if not first(g):
                        dve.wait_ge(stored, g * 16)
                    nc.vector.tensor_tensor(resid_late[:, :, :], nat(B[1]), y2_rest[:, :, :],
                                            ALU.add).then_inc(resid_ready["late"], 1)
                if what == "low":
                    dve.wait_ge(y3_hi, g + 1)
                    nc.vector.scalar_tensor_tensor(part_lo[:, :, :], y3[:, :, :], UP, part_hi[:, :, :], ALU.mult,
                                                   ALU.subtract).then_inc(y3_lo, 1)
                if what == "degree":
                    dve.wait_ge(deg_done, g + 1)
                    nc.vector.tensor_scalar(deg_inv[:, :], degree[:, :], 1.0, None, ALU.max).then_inc(deg_ready, 1)
                    dve.wait_ge(deg_ready, g + 1)
                    nc.vector.reciprocal(deg_inv[:, :], deg_inv[:, :]).then_inc(deg_inv_ready, 1)
                if what == "root":
                    dve.wait_ge(root_done, g * 2 + (n + 1))
                    nc.vector.tensor_tensor(pre[:, :, :], nat(B[1]), row4(("c1", "c2")[n]),
                                            ALU.add).then_inc(root_in, 1)
                if what == "pre":
                    dve.wait_ge(near_w_done, g * 2 + (n + 1))
                    dve.wait_ge(root_in, g * 2 + (n + 1))
                    dve.wait_ge(deg_inv_ready, g + 1)
                    for t in range(TILES):
                        last = nc.vector.scalar_tensor_tensor(pre[:, t, :], nat(B[0])[:, t, :], deg_inv[:, t:t + 1],
                                                              pre[:, t, :], ALU.mult, ALU.add)
                    last.then_inc(pre_ready, 1)
                if what == "elu_low":
                    dve.wait_ge(pre_ready, g * 2 + (n + 1))
                    nc.vector.tensor_scalar(act_out[:, :, :], pre[:, :, :], 0.0, None, ALU.min).then_inc(pre_low, 1)
                if what == "elu":
                    dve.wait_ge(pre_exp, g * 2 + (n + 1))
                    nc.vector.scalar_tensor_tensor(act_out[:, :, :], act_out[:, :, :], -1.0, pre[:, :, :], ALU.add,
                                                   ALU.max).then_inc(elu_ready, 1)
                if what == "part" and n == 0:
                    dve.wait_ge(part_ready, g * 2 + 1)
                    nc.vector.tensor_tensor(y2_rest[:, :, :], act_out[:, :, :], h_parts[0],
                                            ALU.subtract).then_inc(rest1, 1)
                if what == "part" and n == 1:
                    dve.wait_ge(part_ready, g * 2 + 2)
                    nc.vector.tensor_tensor(h_parts[2], y2_rest[:, :, :], h_parts[1],
                                            ALU.subtract).then_inc(part3, 1)
                if what == "resid" and n == 1:
                    dve.wait_ge(elu_ready, g * 2 + 2)
                    nc.vector.tensor_tensor(resid_late[:, :, :], act_out[:, :, :], y3[:, :, :],
                                            ALU.add).then_inc(resid_ready["late"], 1)

            def piece(role, g, p, what, n):
                if role == "next" or what == "no_edge":
                    next_graph(g, p, what, n)
                elif role == "attn":
                    if what != "M":
                        attention(g, p, what, n)
                elif what in NORM:
                    normalise(role, g, what, n)
                elif role == "mid":
                    mid(g, p, what, n)
                else:
                    late(g, p, what, n)

            for what, n in (("proj", 0), ("proj", 1)):
                piece("next", 0, 0, what, n)
            nc.vector.tensor_copy(a_right[:, :], col("a_r").broadcast_to((P, P))).then_inc(gat_a_ready, 1)
            piece("next", 0, 0, "codes", 0)
            dve.wait_ge(rows_in, 16)
            dve.wait_ge(values_zeroed, 4)
            piece("next", 0, 0, "proj", 2)
            dve.wait_ge(weights_in, 16)
            nc.vector.tensor_copy(ident16[:, :], w("ident")).then_inc(dve_consts, 1)
            nc.vector.tensor_scalar(not_self[:, :], w("ident"), -1.0, 1.0, ALU.mult, ALU.add).then_inc(dve_consts, 1)
            dve.wait_ge(dve_consts, 2)
            for what, n in (("codes", 1), ("barred", 0), ("barred", 1), ("barred", 2)):
                piece("next", 0, 0, what, n)
            steps(dve, DVE_ORDER, piece)

        @block.gpsimd
        def _(pool):
            nc.gpsimd.memset(eps_tile[:, :], EPS).then_inc(pool_consts, 1)
            nc.gpsimd.memset(half_tile[:, :], -0.5).then_inc(pool_consts, 1)
            pool.wait_ge(pool_consts, 2)
            nc.gpsimd.memset(q_pack[PACK:SHIFT_ROW + 1, :, :].bitcast(F32), 0.0).then_inc(pack_consts, 1)
            pool.wait_ge(pack_consts, 1)
            nc.gpsimd.memset(k_pack[PACK:SHIFT_ROW + 1, :, :].bitcast(F32), 1.0).then_inc(pack_consts, 1)
            pool.wait_ge(pack_consts, 2)
            pool.wait_ge(rows_in, 16)
            nc.gpsimd.tensor_tensor(ff_bias[:, :], rows[:, ROWS.index("b1"), :], rows[:, ROWS.index("ff2"), :],
                                    ALU.add).then_inc(ff_bias_ready, 1)
            pool.wait_ge(ff_bias_ready, 1)

            def piece(role, g, p, what, n):
                if what == "rstd":
                    per = 4 if role == "mid" else 2
                    pool.wait_ge(moments_ready[role], g * per + (n + 1))
                    nc.gpsimd.tensor_tensor(spread[role][:, :].rearrange("p (t o) -> p t o", o=1),
                                            moments[role][:, :, 1:2],
                                            eps_tile[:, :].rearrange("p (t o) -> p t o", o=1),
                                            ALU.add).then_inc(spread_ready[role], 1)
                    pool.wait_ge(spread_ready[role], g * per + (n + 1))
                    nc.gpsimd.tensor_tensor(rstd[role][:, :], spread[role][:, :], half_tile[:, :],
                                            ALU.pow).then_inc(rstd_ready[role], 1)
                if what == "x":
                    pool.wait_ge(x_loaded, g * 16 + 16)
                    if not first(g):
                        pool.wait_ge(resid_ready["mid"], g * 4)
                    nc.gpsimd.tensor_tensor(x_bo_y1[:, :, :], x_nat[:, :, :], row4("bo"), ALU.add).then_inc(x_bo_ready, 1)
                    nc.gpsimd.tensor_tensor(x_b2[:, :, :], x_nat[:, :, :], row4("b2"), ALU.add).then_inc(x_b2_ready, 1)
                if what == "x1":
                    pool.wait_ge(normed["mid"], g * 4 + 1)
                    if not first(g):
                        pool.wait_ge(lo_ready, g)
                    nc.gpsimd.tensor_tensor(x1_y2[:, :, :], z_mid[:, :, :], row4("g1"), ALU.mult).then_inc(z_scaled, 1)
                    pool.wait_ge(z_scaled, g + 1)
                    nc.gpsimd.tensor_tensor(x1_y2[:, :, :], x1_y2[:, :, :],
                                            ff_bias[:, :].rearrange("p (o c) -> p o c", o=1)
                                            .broadcast_to((P, TILES, DIM)), ALU.add).then_inc(x1_ready, 1)
                if what == "y1":
                    pool.wait_ge(normed["mid"], g * 4 + 2)
                    nc.gpsimd.tensor_tensor(z_mid[:, :, :], z_mid[:, :, :], row4("g2"), ALU.mult).then_inc(z2_scaled, 1)
                    pool.wait_ge(z2_scaled, g + 1)
                    nc.gpsimd.tensor_tensor(resid_mid[:, :, :], z_mid[:, :, :], x_b2[:, :, :],
                                            ALU.add).then_inc(resid_ready["mid"], 1)
                if what == "y2":
                    pool.wait_ge(normed["mid"], g * 4 + 4)
                    if not first(g):
                        pool.wait_ge(part3, g)
                    nc.gpsimd.tensor_tensor(y2_rest[:, :, :], x1_y2[:, :, :], row4("bias"), ALU.add).then_inc(y2_bias, 1)

            steps(pool, POOL_ORDER, piece)


_INPUTS = ("x", "xT", "adj", "adjT", "weights", "vec_rows", "vec_cols")


def kernel(**inputs):
    import numpy as np
    import concourse.bacc as bacc
    from concourse.bass_utils import run_bass_kernel_spmd

    a = {k: np.asarray(v) for k, v in inputs.items()}
    lay = np.ascontiguousarray
    f32 = np.float32

    def tiled(m):
        return lay(m.reshape(GRAPHS, TILES, P, m.shape[2]).transpose(0, 2, 1, 3)).reshape(GRAPHS, P, -1)

    wqkv = a["L0_gnn_Wqkv"]
    pieces = {
        "q": wqkv[0:DIM].T, "k": wqkv[DIM:2 * DIM].T, "v": wqkv[2 * DIM:].T, "o": a["L0_gnn_Wo"].T,
        "ff1": a["L0_gnn_W1"].T,
        "ff2": a["L0_gnn_W2"].T.reshape(FT, P, DIM).transpose(1, 0, 2).reshape(P, FT * DIM),
        "gat": a["L1_gnn_W"], "gatT": a["L1_gnn_W"].T,
        "rel": a["L2_gnn_weight"].transpose(1, 0, 2).reshape(P, RELS * DIM),
        "root1": a["L3_gnn_w_root1"], "near1": a["L3_gnn_w_rel1"][1],
        "root2": a["L3_gnn_w_root2"], "near2": a["L3_gnn_w_rel2"][1],
        "ident": np.eye(P, dtype=f32),
    }
    bqkv = a["L0_gnn_bqkv"]
    vec = {
        "bq": bqkv[0:DIM], "bk": bqkv[DIM:2 * DIM], "bv": bqkv[2 * DIM:], "bo": a["L0_gnn_bo"],
        "g1": a["L0_gnn_ln1_g"], "b1": a["L0_gnn_ln1_b"], "g2": a["L0_gnn_ln2_g"], "b2": a["L0_gnn_ln2_b"],
        "ff2": a["L0_gnn_b2"], "bias": a["L2_gnn_bias"], "c1": a["L3_gnn_b1"], "c2": a["L3_gnn_b2"],
        "a_l": a["L1_gnn_a"][0:DIM, 0], "a_r": a["L1_gnn_a"][DIM:, 0],
    }
    for f in range(FT):
        vec[f"ff1_{f}"] = a["L0_gnn_b1"][f * P:(f + 1) * P]
    arrays = {
        "x": tiled(a["x"]), "xT": lay(a["x"].transpose(0, 2, 1)),
        "adj": tiled(a["adj"]), "adjT": tiled(a["adj"].transpose(0, 2, 1)),
        "weights": lay(np.concatenate([pieces[n] for n in W_COLS], axis=1)),
        "vec_rows": lay(np.concatenate([vec[n] for n in ROWS])),
        "vec_cols": lay(np.stack([vec[n] for n in VECS], axis=1)),
    }
    nc = bacc.Bacc("TRN2", target_bir_lowering=False, num_devices=1)
    args = [nc.dram_tensor(n, arrays[n].shape, mybir.dt.from_np(arrays[n].dtype), kind="ExternalInput").ap()
            for n in _INPUTS]
    out = nc.dram_tensor("out", (GRAPHS, P, TILES * DIM), F32, kind="ExternalOutput").ap()
    build(nc, *args, out)
    got = run_bass_kernel_spmd(nc, [arrays], core_ids=[0]).results[0]["out"]
    return got.reshape(GRAPHS, P, TILES, DIM).transpose(0, 2, 1, 3).reshape(GRAPHS, NODES, DIM)
```
